# Optimizing a Trainium2 kernel written in Bass

```python
import numpy as np
import jax
import jax.numpy as jnp

def _softmax(x, axis=-1):
    return jax.nn.softmax(x, axis=axis)
def _gelu(x):
    return jax.nn.gelu(x, approximate=True)
def _silu(x):
    return jax.nn.silu(x)
def _sigmoid(x):
    return jax.nn.sigmoid(x)
def _layernorm(x, axis=-1, eps=1e-5):
    m = jnp.mean(x, axis=axis, keepdims=True)
    v = jnp.var(x, axis=axis, keepdims=True)
    return (x - m) / jnp.sqrt(v + eps)
def _scatter_add(tgt, idx, src, axis=0):
    return tgt.at[idx].add(src)
def _segment_sum(src, seg, n):
    return jax.ops.segment_sum(src, seg, n)

kernel_name = 'mk_adj_resnorm_d2_adj_512_899bd4'

def setup_inputs(seed: int = 0):
    np.random.seed(seed)
    _w = jnp.asarray
    def _rec_inputs():
        import jax
        import jax.numpy as jnp
        _gk = jax.random.key(seed)
        x = -0.0003929 + 0.9999 * jax.random.normal(jax.random.fold_in(_gk, 1), (32, 512, 512), jnp.float32)
        _a = jax.random.bernoulli(jax.random.fold_in(_gk, 2), 0.03125, (512, 512))
        _a = jnp.logical_or(_a, jnp.eye(512, dtype=bool))
        _af = _a.astype(jnp.float32)
        _af = _af * jax.random.uniform(jax.random.fold_in(_gk, 3), (512, 512), jnp.float32, 0.05, 1)
        adj = _af
        return x, adj
    x, adj = _rec_inputs()
    def _L0_gnn_setup():
        import jax, jax.numpy as jnp
        import numpy as np
        B, N, D, O = (8, 4096, 512, 512)
        key = jax.random.key(seed)
        k1, k2, k3, k4 = jax.random.split(key, 4)
        x = jax.random.normal(k1, (B, N, D), dtype=jnp.float32)
        adj = jax.random.uniform(k2, (N, N), dtype=jnp.float32)
        weight = jax.random.normal(k3, (D, O), dtype=jnp.float32) * 0.02
        bias = jax.random.normal(k4, (O,), dtype=jnp.float32) * 0.02
        return {'x': x, 'adj': adj, 'weight': weight, 'bias': bias}
    _L0_gnn_all = _L0_gnn_setup()
    _L0_gnn_in = {k: v for k, v in _L0_gnn_all.items() if k in ('weight', 'bias', )}
    del _L0_gnn_all

    def _L1_gnn_setup():
        import jax, jax.numpy as jnp
        import numpy as np
        B, N, D, H = (16, 1025, 512, 8)
        LN_EPS = 1e-05

        def _make_mask(key, n):
            n_proto = n - 1
            adj = jax.random.bernoulli(key, 0.03, (n_proto, n_proto)).astype(jnp.float32)
            adj = jnp.clip(adj + adj.T + jnp.eye(n_proto, dtype=jnp.float32), 0.0, 1.0)
            mask = jnp.zeros((n, n), dtype=jnp.float32)
            mask = mask.at[0, :].set(1.0).at[:, 0].set(1.0)
            mask = mask.at[1:, 1:].set(adj)
            return mask
        key = jax.random.key(seed)
        ks = jax.random.split(key, 7)
        s = 1.0 / np.sqrt(D)
        return {'x': jax.random.normal(ks[0], (B, N, D), dtype=jnp.float32), 'w_qkv': jax.random.uniform(ks[1], (D, 3 * D), dtype=jnp.float32, minval=-s, maxval=s), 'w_proj': jax.random.uniform(ks[2], (D, D), dtype=jnp.float32, minval=-s, maxval=s), 'b_proj': jnp.zeros((D,), dtype=jnp.float32), 'ln_gamma': jnp.ones((D,), dtype=jnp.float32), 'ln_beta': jnp.zeros((D,), dtype=jnp.float32), 'attn_mask': _make_mask(ks[3], N)}
    _L1_gnn_all = _L1_gnn_setup()
    _L1_gnn_in = {k: v for k, v in _L1_gnn_all.items() if k in ('w_qkv', 'w_proj', 'b_proj', 'ln_gamma', 'ln_beta', )}
    del _L1_gnn_all

    return {
        "x": x,
        "adj": adj,
        "L0_gnn_weight": _L0_gnn_in["weight"],
        "L0_gnn_bias": _L0_gnn_in["bias"],
        "L1_gnn_w_qkv": _L1_gnn_in["w_qkv"],
        "L1_gnn_w_proj": _L1_gnn_in["w_proj"],
        "L1_gnn_b_proj": _L1_gnn_in["b_proj"],
        "L1_gnn_ln_gamma": _L1_gnn_in["ln_gamma"],
        "L1_gnn_ln_beta": _L1_gnn_in["ln_beta"],
    }

def reference(x, adj, L0_gnn_weight, L0_gnn_bias, L1_gnn_w_qkv, L1_gnn_w_proj, L1_gnn_b_proj, L1_gnn_ln_gamma, L1_gnn_ln_beta):
    import jax
    import jax.numpy as jnp
    def _L0_gnn_ref(x, adj, weight, bias):
        import jax, jax.numpy as jnp
        import numpy as np
        B, N, D, O = (8, 4096, 512, 512)
        y = jnp.einsum('nm,bmd->bnd', adj, x)
        out = jnp.einsum('bnd,do->bno', y, weight) + bias
        return out

    def _L1_gnn_ref(x, w_qkv, w_proj, b_proj, ln_gamma, ln_beta, attn_mask):
        import jax, jax.numpy as jnp
        import numpy as np
        B, N, D, H = (16, 1025, 512, 8)
        LN_EPS = 1e-05

        def _make_mask(key, n):
            n_proto = n - 1
            adj = jax.random.bernoulli(key, 0.03, (n_proto, n_proto)).astype(jnp.float32)
            adj = jnp.clip(adj + adj.T + jnp.eye(n_proto, dtype=jnp.float32), 0.0, 1.0)
            mask = jnp.zeros((n, n), dtype=jnp.float32)
            mask = mask.at[0, :].set(1.0).at[:, 0].set(1.0)
            mask = mask.at[1:, 1:].set(adj)
            return mask
        b, n, d = x.shape
        hd = d // H
        scale = hd ** (-0.5)
        qkv = (x @ w_qkv).reshape(b, n, 3, H, hd).transpose(2, 0, 3, 1, 4)
        q, k, v = (qkv[0], qkv[1], qkv[2])
        attn = jnp.einsum('bhnd,bhmd->bhnm', q, k) * scale
        attn = jnp.where(attn_mask[None, None] == 0, -jnp.inf, attn)
        attn = jax.nn.softmax(attn, axis=-1)
        o = jnp.einsum('bhnm,bhmd->bhnd', attn, v).transpose(0, 2, 1, 3).reshape(b, n, d)
        o = o @ w_proj + b_proj
        mu = jnp.mean(o, axis=-1, keepdims=True)
        var = jnp.mean(jnp.square(o - mu), axis=-1, keepdims=True)
        ln = (o - mu) * jax.lax.rsqrt(var + LN_EPS) * ln_gamma + ln_beta
        return o + ln

    x = _layernorm(x + _L0_gnn_ref(x, adj, L0_gnn_weight, L0_gnn_bias), axis=-1)
    x = _layernorm(x + _L1_gnn_ref(x, L1_gnn_w_qkv, L1_gnn_w_proj, L1_gnn_b_proj, L1_gnn_ln_gamma, L1_gnn_ln_beta, adj), axis=-1)
    return x


_drawn_inputs = setup_inputs


def setup_inputs(seed=0):
    import zlib

    import numpy as np

    out = dict(_drawn_inputs(seed))
    spreads = {'L1_gnn_b_proj': (0.0, 0.1), 'L1_gnn_ln_gamma': (1.0, 0.2), 'L1_gnn_ln_beta': (0.0, 0.1)}
    factors = {}
    for name, (base, spread) in spreads.items():
        noise = np.random.default_rng([zlib.crc32(name.encode()), seed]).standard_normal(out[name].shape)
        drawn = base * np.exp(spread * noise) if base else spread * noise
        out[name] = jnp.asarray(drawn.astype(out[name].dtype))
    for name, factor in factors.items():
        out[name] = (out[name] * factor).astype(out[name].dtype)
    return out
```

```python
from contextlib import ExitStack

import concourse.bass as bass
from concourse import mybir

F32 = mybir.dt.float32
F32R = mybir.dt.float32r
BF16 = mybir.dt.bfloat16
ALU = mybir.AluOpType
ACT = mybir.ActivationFunctionType
P = 128
EPS = 1e-5
MASKED = -1.0e30


def graph_layers(nc, x, adj, w0, b0, wqkv, wproj, bproj, gamma, beta, out):
    B, N, D = x.shape
    T = N // P
    HEAD = 64
    PAIRS = D // (2 * HEAD)
    SCALE = float(HEAD) ** -0.5
    assert N == 512 and D == 512 and T == 4 and PAIRS == 4

    u_dram = nc.dram_tensor("u_rows", [B, N, D], F32, kind="Internal").ap()
    uth_dram = nc.dram_tensor("ut_hi", [B, P, T, N], F32, kind="Internal").ap()
    utl_dram = nc.dram_tensor("ut_lo", [B, P, T, N], F32, kind="Internal").ap()

    def rows(m):
        return m.rearrange("(t p) d -> p t d", p=P)

    def f32(ap):
        return ap.bitcast(F32)

    with ExitStack() as whole:
        def keep(name, shape, dt):
            return whole.enter_context(nc.sbuf_tensor(name, shape, dt))

        w_hi = keep("w_hi", [P, 4, T, D], F32R)
        w_lo = keep("w_lo", [P, 4, T, D], F32R)
        mask_bias = keep("mask_bias", [P, T, N], BF16)
        ident = keep("ident", [P, P], F32)
        half_neg = keep("half_neg", [P, 1], F32)
        bproj_row = keep("bproj_row", [P, D], F32)
        gamma_row = keep("gamma_row", [P, D], F32)
        beta_row = keep("beta_row", [P, D], F32)

        psum = [whole.enter_context(nc.psum_tensor(f"bank{i}", [P, 512], F32)) for i in range(8)]

        with ExitStack() as first:
            def sb(name, shape, dt):
                return first.enter_context(nc.sbuf_tensor(name, shape, dt))

            def sem(name):
                return first.enter_context(nc.semaphore(name))

            adjt_hi = sb("adjt_hi", [P, T, N], F32R)
            adjt_lo = sb("adjt_lo", [P, T, N], F32R)
            w0_hi = sb("w0_hi", [P, T, D], F32R)
            w0_lo = sb("w0_lo", [P, T, D], F32R)
            b0_row = sb("b0_row", [P, 1, D], F32)
            x_in = sb("x_in", [P, T, D], F32)
            xb = sb("xb", [P, T, D], F32)
            x_hi = sb("x_hi", [P, T, D], F32R)
            x_lo = sb("x_lo", [P, T, D], F32R)
            yt_hi = sb("yt_hi", [P, T, N], F32R)
            yt_lo = sb("yt_lo", [P, T, N], F32R)
            res = sb("res", [P, 2, D], F32)
            u = sb("u", [P, T, D], F32)
            ut_hi = sb("ut_hi_sb", [P, T, N], F32R)
            ut_lo = sb("ut_lo_sb", [P, T, N], F32R)
            stats = sb("stats", [P, T, 6], F32)
            mean_var = sb("mean_var", [P, T, 2], F32)
            var_eps = sb("var_eps", [P, T], F32)
            rstd = sb("rstd", [P, T], F32)
            shift = sb("shift", [P, T], F32)

            stage = [x_in, xb, u]
            ident_made = sem("ident_made")
            rows_in = sem("rows_in")
            chunk_in = [sem(f"chunk_in{i}") for i in range(3)]
            hi_made = sem("hi_made")
            lo_made = sem("lo_made")
            adj_turned = sem("adj_turned")
            adjt_hi_made = sem("adjt_hi_made")
            adjt_lo_made = sem("adjt_lo_made")
            mask_made = sem("mask_made")

            sources = [rows(adj), rows(w0)] + [rows(wqkv[:, i * D:(i + 1) * D]) for i in range(3)] + [rows(wproj)]
            parts = [None, (w0_hi[:], w0_lo[:])] + [(w_hi[:, i], w_lo[:, i]) for i in range(4)]

            with nc.Block() as block:
                @block.sync
                def _(sp):
                    for c in range(6):
                        if c == 3:
                            sp.wait_ge(adj_turned, T)
                            sp.wait_ge(mask_made, 1)
                        elif c > 3:
                            sp.wait_ge(lo_made, c - 3)
                        sp.dma_start(stage[c % 3][:], sources[c]).then_inc(chunk_in[c % 3], 16)
                    for row, src in ((b0_row[:, 0, :], b0), (bproj_row[:], bproj), (gamma_row[:], gamma),
                                     (beta_row[:], beta)):
                        sp.dma_start(row, src.partition_broadcast(P)).then_inc(rows_in, 16)
                    sp.wait_ge(rows_in, 64)

                @block.gpsimd
                def _(pool):
                    pool.memset(half_neg[:], -0.5)
                    pool.memset(ident[:], 0.0).then_inc(ident_made, 1)
                    pool.wait_ge(ident_made, 1)
                    pool.affine_select(out=ident[:], in_=ident[:], compare_op=ALU.not_equal, fill=1.0, base=0,
                                       pattern=[[-1, P]], channel_multiplier=1).then_inc(ident_made, 1)

                @block.tensor
                def _(pe):
                    pe.wait_ge(ident_made, 2)
                    pe.wait_ge(chunk_in[0], 16)
                    for m in range(T):
                        for n in range(T):
                            last = pe.transpose(psum[m][:, n * P:(n + 1) * P], stage[0][:, n, m * P:(m + 1) * P],
                                                ident[:])
                        last.then_inc(adj_turned, 1)

                @block.scalar
                def _(act):
                    for m in range(T):
                        act.wait_ge(adj_turned, m + 1)
                        act.activation(adjt_hi[:, m, :], psum[m][:], ACT.Copy).then_inc(adjt_hi_made, 1)
                    for c in range(1, 6):
                        act.wait_ge(chunk_in[c % 3], 16 * (c // 3 + 1))
                        act.activation(parts[c][0], stage[c % 3][:], ACT.Copy).then_inc(hi_made, 1)

                @block.vector
                def _(dve):
                    dve.wait_ge(chunk_in[0], 16)
                    dve.tensor_scalar(mask_bias[:], stage[0][:], 0.0, MASKED, ALU.is_equal, ALU.mult)\
                        .then_inc(mask_made, 1)
                    for m in range(T):
                        dve.wait_ge(adjt_hi_made, m + 1)
                        dve.tensor_tensor(adjt_lo[:, m, :], psum[m][:], f32(adjt_hi[:, m, :]), ALU.subtract)\
                            .then_inc(adjt_lo_made, 1)
                    for c in range(1, 6):
                        dve.wait_ge(hi_made, c)
                        dve.tensor_tensor(parts[c][1], stage[c % 3][:], f32(parts[c][0]), ALU.subtract)\
                            .then_inc(lo_made, 1)

            x_loaded = sem("x_loaded")
            xhi_made = sem("xhi_made")
            xlo_made = sem("xlo_made")
            xb_made = sem("xb_made")
            yz_done = sem("yz_done")
            yhi_made = sem("yhi_made")
            ylo_made = sem("ylo_made")
            res_made = sem("res_made")
            stats_made = sem("stats_made")
            mean_made = sem("mean_made")
            eps_added = sem("eps_added")
            rstd_made = sem("rstd_made")
            shift_made = sem("shift_made")
            u_made = sem("u_made")
            u_turned = sem("u_turned")
            uthi_made = sem("uthi_made")
            utlo_made = sem("utlo_made")
            u_stored = sem("u_stored")
            ut_stored = sem("ut_stored")

            yz_bank = psum[0:4]
            turn_bank = psum[4:6]

            with nc.Block() as block:
                @block.sync
                def _(sp):
                    def store_ut(b):
                        sp.wait_ge(utlo_made, b * 4 + 4)
                        sp.dma_start(uth_dram[b], f32(ut_hi[:])).then_inc(ut_stored, 16)
                        sp.dma_start(utl_dram[b], f32(ut_lo[:])).then_inc(ut_stored, 16)

                    def store_u(b):
                        sp.wait_ge(u_made, b * 4 + 4)
                        sp.dma_start(rows(u_dram[b]), u[:]).then_inc(u_stored, 16)

                    def load_x(b):
                        sp.wait_ge(xb_made, b)
                        sp.wait_ge(xlo_made, b)
                        sp.dma_start(x_in[:], rows(x[b])).then_inc(x_loaded, 16)

                    sp.dma_start(x_in[:], rows(x[0])).then_inc(x_loaded, 16)
                    load_x(1)
                    store_u(0)
                    with sp.Fori(1, B - 1, 1) as b:
                        load_x(b + 1)
                        store_ut(b - 1)
                        store_u(b)
                    store_ut(B - 2)
                    store_u(B - 1)
                    store_ut(B - 1)
                    sp.wait_ge(u_stored, 16 * B)
                    sp.wait_ge(ut_stored, 32 * B)

                @block.gpsimd
                def _(pool):
                    def batch(b, first=False):
                        pool.wait_ge(x_loaded, b * 16 + 16)
                        if not first:
                            pool.wait_ge(res_made, b * 4)
                        pool.tensor_tensor(xb[:], x_in[:], b0_row[:].to_broadcast((P, T, D)), ALU.add)\
                            .then_inc(xb_made, 1)
                        for j in range(T):
                            pool.wait_ge(eps_added, b * 4 + (j + 1))
                            pool.tensor_tensor(rstd[:, j:j + 1], var_eps[:, j:j + 1], half_neg[:], ALU.pow)\
                                .then_inc(rstd_made, 1)

                    batch(0, first=True)
                    with pool.Fori(1, B, 1) as b:
                        batch(b)

                @block.tensor
                def _(pe):
                    def y(b, j, first=False):
                        bank = yz_bank[j]
                        if j == 0:
                            pe.wait_ge(xlo_made, b + 1)
                        if not first:
                            pe.wait_ge(res_made, b * 4 + (j - 3))
                        n = 0
                        for a, c in ((x_hi, adjt_hi), (x_hi, adjt_lo), (x_lo, adjt_hi)):
                            for m in range(T):
                                last = pe.matmul(bank[:], a[:, m, j * P:(j + 1) * P], c[:, m, :],
                                                 start=n == 0, stop=n == 11)
                                n += 1
                        last.then_inc(yz_done, 1)

                    def z(b, j):
                        bank = yz_bank[j]
                        for m in range(T):
                            if j == 0:
                                pe.wait_ge(ylo_made, b * 4 + (m + 1))
                            for i, (a, c) in enumerate(((yt_hi, w0_hi), (yt_hi, w0_lo), (yt_lo, w0_hi))):
                                last = pe.matmul(bank[:], a[:, m, j * P:(j + 1) * P], c[:, m, :],
                                                 start=m == 0 and i == 0, stop=m == 3 and i == 2)
                        last.then_inc(yz_done, 1)

                    def turn(b, j, free=True):
                        pe.wait_ge(u_made, b * 4 + (j + 1))
                        if free:
                            pe.wait_ge(utlo_made, b * 4 + (j - 1))
                        for d in range(T):
                            last = pe.transpose(turn_bank[j % 2][:, d * P:(d + 1) * P], u[:, j, d * P:(d + 1) * P],
                                                ident[:])
                        last.then_inc(u_turned, 1)

                    def batch(b, first=False):
                        y(b, 0, first)
                        y(b, 1, first)
                        if not first:
                            turn(b - 1, 3)
                        y(b, 2, first)
                        y(b, 3, first)
                        z(b, 0)
                        z(b, 1)
                        turn(b, 0, free=not first)
                        z(b, 2)
                        turn(b, 1, free=not first)
                        z(b, 3)
                        turn(b, 2)

                    batch(0, first=True)
                    with pe.Fori(1, B, 1) as b:
                        batch(b)
                    turn(B - 1, 3)

                @block.scalar
                def _(act):
                    def x_hi_part(b):
                        act.wait_ge(x_loaded, b * 16 + 16)
                        act.activation(x_hi[:], x_in[:], ACT.Copy).then_inc(xhi_made, 1)

                    def y_hi_part(b, j):
                        act.wait_ge(yz_done, b * 8 + (j + 1))
                        act.activation(yt_hi[:, j, :], yz_bank[j][:], ACT.Copy).then_inc(yhi_made, 1)

                    def normalise(b, j):
                        act.wait_ge(shift_made, b * 4 + (j + 1))
                        act.activation(u[:, j, :], res[:, j % 2, :], ACT.Identity, bias=shift[:, j:j + 1],
                                       scale=rstd[:, j:j + 1]).then_inc(u_made, 1)

                    def ut_hi_part(b, j):
                        act.wait_ge(u_turned, b * 4 + (j + 1))
                        act.activation(ut_hi[:, :, j * P:(j + 1) * P],
                                       turn_bank[j % 2][:].rearrange("p (d n) -> p d n", d=T), ACT.Copy)\
                            .then_inc(uthi_made, 1)

                    def batch(b, first=False, last=False):
                        y_hi_part(b, 0)
                        y_hi_part(b, 1)
                        if not first:
                            ut_hi_part(b - 1, 3)
                        y_hi_part(b, 2)
                        y_hi_part(b, 3)
                        if not last:
                            x_hi_part(b + 1)
                        if not first:
                            act.wait_ge(u_stored, b * 16)
                            act.wait_ge(u_turned, b * 4)
                        normalise(b, 0)
                        normalise(b, 1)
                        if not first:
                            act.wait_ge(ut_stored, b * 32)
                        ut_hi_part(b, 0)
                        normalise(b, 2)
                        ut_hi_part(b, 1)
                        normalise(b, 3)
                        ut_hi_part(b, 2)

                    x_hi_part(0)
                    batch(0, first=True)
                    with act.Fori(1, B - 1, 1) as b:
                        batch(b)
                    batch(B - 1, last=True)
                    ut_hi_part(B - 1, 3)

                @block.vector
                def _(dve):
                    def x_lo_part(b):
                        dve.wait_ge(xhi_made, b + 1)
                        dve.tensor_tensor(x_lo[:], x_in[:], f32(x_hi[:]), ALU.subtract).then_inc(xlo_made, 1)

                    def y_lo_part(b, j):
                        dve.wait_ge(yhi_made, b * 4 + (j + 1))
                        dve.tensor_tensor(yt_lo[:, j, :], yz_bank[j][:], f32(yt_hi[:, j, :]), ALU.subtract)\
                            .then_inc(ylo_made, 1)

                    def row_stats(b, j, free=True):
                        dve.wait_ge(yz_done, b * 8 + (j + 5))
                        if j == 0:
                            dve.wait_ge(xb_made, b + 1)
                        if free:
                            dve.wait_ge(u_made, b * 4 + (j - 1))
                        dve.tensor_tensor(res[:, j % 2, :], yz_bank[j][:], xb[:, j, :], ALU.add)\
                            .then_inc(res_made, 1)
                        dve.wait_ge(res_made, b * 4 + (j + 1))
                        dve.bn_stats(stats[:, j, :], res[:, j % 2, :]).then_inc(stats_made, 1)
                        dve.wait_ge(stats_made, 1)
                        dve.wait_ge(stats_made, b * 4 + (j + 1))
                        dve.bn_aggr(mean_var[:, j, :], stats[:, j, :]).then_inc(mean_made, 1)
                        dve.wait_ge(mean_made, b * 4 + (j + 1))
                        dve.tensor_scalar(var_eps[:, j:j + 1], mean_var[:, j, 1:2], EPS, None, ALU.add)\
                            .then_inc(eps_added, 1)

                    def row_shift(b, j):
                        dve.wait_ge(rstd_made, b * 4 + (j + 1))
                        dve.tensor_scalar(shift[:, j:j + 1], mean_var[:, j, 0:1], rstd[:, j:j + 1], -1.0,
                                          ALU.mult, ALU.mult).then_inc(shift_made, 1)

                    def ut_lo_part(b, j):
                        dve.wait_ge(uthi_made, b * 4 + (j + 1))
                        cols = slice(j * P, (j + 1) * P)
                        dve.tensor_tensor(ut_lo[:, :, cols], turn_bank[j % 2][:].rearrange("p (d n) -> p d n", d=T),
                                          f32(ut_hi[:, :, cols]), ALU.subtract).then_inc(utlo_made, 1)

                    def batch(b, first=False, last=False):
                        y_lo_part(b, 0)
                        y_lo_part(b, 1)
                        if not first:
                            ut_lo_part(b - 1, 3)
                        y_lo_part(b, 2)
                        y_lo_part(b, 3)
                        if not last:
                            x_lo_part(b + 1)
                        for j in range(T):
                            row_stats(b, j, free=j >= 2 or not first)
                            row_shift(b, j)
                            if j > 0:
                                ut_lo_part(b, j - 1)

                    x_lo_part(0)
                    batch(0, first=True)
                    with dve.Fori(1, B - 1, 1) as b:
                        batch(b)
                    batch(B - 1, last=True)
                    ut_lo_part(B - 1, 3)

        with ExitStack() as second:
            def sb(name, shape, dt):
                return second.enter_context(nc.sbuf_tensor(name, shape, dt))

            def sem(name):
                return second.enter_context(nc.semaphore(name))

            xt_hi = sb("xt_hi", [P, T, N], F32R)
            xt_lo = sb("xt_lo", [P, T, N], F32R)
            q_hi = sb("q_hi", [P, PAIRS, N], F32R)
            q_lo = sb("q_lo", [P, PAIRS, N], F32R)
            k_hi = sb("k_hi", [P, PAIRS, N], F32R)
            k_lo = sb("k_lo", [P, PAIRS, N], F32R)
            v = sb("v", [P, T, 2 * PAIRS, 2, HEAD], F32R)
            probs = sb("probs", [P, 2, 2, N], F32)
            pt_hi = sb("pt_hi", [P, 2, T, N], F32R)
            pt_lo = sb("pt_lo", [P, 2, T, N], F32R)
            ot_hi = sb("ot_hi", [P, PAIRS, N], F32R)
            ot_lo = sb("ot_lo", [P, PAIRS, N], F32R)
            ot = sb("ot", [P, N], F32)
            o = sb("o", [P, T, D], F32)
            t = sb("t", [P, D], F32)
            bias_row = sb("bias_row", [P, 4, 2], F32)
            sums = sb("sums", [P, 4, 2], F32)
            inv_sums = sb("inv_sums", [P, 4, 2], F32)
            stats = sb("o_stats", [P, T, 2, 6], F32)
            mean_var = sb("o_mean_var", [P, T, 2, 2], F32)
            var_eps = sb("o_var_eps", [P, T, 2], F32)
            rstd = sb("o_rstd", [P, T, 2], F32)
            shift = sb("o_shift", [P, T, 2], F32)

            s_bank, t_bank, o_bank, g_bank = psum[0:2], psum[2:4], psum[4:6], psum[6:8]

            STEPS = PAIRS * T
            STRIP = 32
            scores_made = sem("scores_made")
            max_found = sem("max_found")
            exp_made = sem("exp_made")
            inv_made = sem("inv_made")
            probs_made = sem("probs_made")
            probs_turned = sem("probs_turned")
            pthi_made = sem("pthi_made")
            ptlo_made = sem("ptlo_made")
            pv_done = sem("pv_done")
            ot_half = sem("ot_half")
            ot_summed = sem("ot_summed")
            othi_made = sem("othi_made")
            otlo_made = sem("otlo_made")
            xt_loaded = sem("xt_loaded")
            qkv_done = sem("qkv_done")
            qkvhi_made = sem("qkvhi_made")
            qkvlo_made = sem("qkvlo_made")
            proj_done = sem("proj_done")
            o_made = sem("o_made")
            stats_made = [sem(f"o_stats_made{i}") for i in range(2)]
            mean_made = [sem(f"o_mean_made{i}") for i in range(2)]
            eps_added = [sem(f"o_eps_added{i}") for i in range(2)]
            rstd_made = [sem(f"o_rstd_made{i}") for i in range(2)]
            shift_made = [sem(f"o_shift_made{i}") for i in range(2)]
            ln_made = sem("ln_made")
            gamma_done = sem("gamma_done")
            beta_done = sem("beta_done")
            o_added = sem("o_added")
            u_loaded = sem("u_loaded")
            u_added = sem("u_added")
            y_made = sem("y_made")
            y_stored = sem("y_stored")

            QK = 2 * PAIRS
            unit_step = [4 + (12 * (i + 1) + 7) // 8 - 1 for i in range(QK)]
            ln_step = {2 + 3 * n: n for n in range(T)}

            with nc.Block() as block:
                @block.sync
                def _(sp):
                    def load_xt(b, first=False):
                        if not first:
                            sp.wait_ge(qkv_done, b * 12)
                        sp.dma_start(f32(xt_hi[:]), uth_dram[b]).then_inc(xt_loaded, 16)
                        sp.dma_start(f32(xt_lo[:]), utl_dram[b]).then_inc(xt_loaded, 16)

                    def finish(b):
                        for n in range(T):
                            sp.wait_ge(o_added, b * 4 + (n - 3))
                            sp.dma_start(o[:, n, :], u_dram[b - 1, n * P:(n + 1) * P, :]).then_inc(u_loaded, 16)
                            sp.wait_ge(y_made, b * 4 + (n - 3))
                            sp.dma_start(out[b - 1, n * P:(n + 1) * P, :], o[:, n, :]).then_inc(y_stored, 16)

                    load_xt(0, first=True)
                    load_xt(1)
                    with sp.Fori(1, B - 1, 1) as b:
                        load_xt(b + 1)
                        finish(b)
                    finish(B - 1)
                    finish(B)
                    sp.wait_ge(y_stored, 64 * B)

                @block.gpsimd
                def _(pool):
                    def normalise(b, k):
                        pool.wait_ge(inv_made, b * STEPS + (k + 1))
                        strip, rest = slice(0, STRIP), slice(STRIP, N)
                        pool.tensor_tensor(probs[:, k % 2, 0, strip], probs[:, k % 2, 0, strip],
                                           inv_sums[:, k % 4, 0:1].to_broadcast((P, STRIP)), ALU.mult)
                        for a, cols in ((0, rest), (1, slice(0, N))):
                            pool.tensor_scalar(probs[:, k % 2, a, cols], probs[:, k % 2, a, cols],
                                               inv_sums[:, k % 4, a:a + 1], 0.0, ALU.mult, ALU.add)\
                                .then_inc(probs_made, 1)

                    def power(b, n, i):
                        pool.wait_ge(eps_added[i], b * 4 + (n - 3))
                        pool.tensor_tensor(rstd[:, n, i:i + 1], var_eps[:, n, i:i + 1], half_neg[:], ALU.pow)\
                            .then_inc(rstd_made[i], 1)

                    def times_gamma(b, n):
                        pool.wait_ge(ln_made, b * 4 + (n - 3))
                        pool.tensor_tensor(t[:], t[:], gamma_row[:], ALU.mult).then_inc(gamma_done, 1)

                    def batch(b, attend=True, last_part=True, more=True):
                        for k in range(STEPS):
                            if attend and (k + 1 < STEPS or more):
                                normalise(b, k + 1)
                            if last_part:
                                if k < T:
                                    power(b, k, 0)
                                if k - 2 in ln_step:
                                    power(b, ln_step[k - 2], 1)
                                if k in ln_step:
                                    times_gamma(b, ln_step[k])

                    normalise(0, 0)
                    batch(0, last_part=False)
                    with pool.Fori(1, B - 1, 1) as b:
                        batch(b)
                    batch(B - 1, more=False)
                    batch(B, attend=False)

                @block.tensor
                def _(pe):
                    def scores(b, k):
                        pair, n = k // T % PAIRS, k % T
                        if n == 0:
                            pe.wait_ge(qkvlo_made, (b + k // STEPS) * 12 + (2 * pair + 2))
                        parts = ((q_hi, k_hi), (q_hi, k_lo), (q_lo, k_hi))
                        for a in range(2):
                            if not (isinstance(b, int) and b * STEPS + k == 0):
                                pe.wait_ge(max_found, b * 32 + (2 * k + a - 1))
                        for i, (l, r) in enumerate(parts):
                            for a in range(2):
                                h = slice(a * HEAD, (a + 1) * HEAD)
                                last = pe.matmul(s_bank[a][:], l[h, pair, n * P:(n + 1) * P], r[h, pair, :],
                                                 start=i == 0, stop=i == 2)
                                if i == 2:
                                    last.then_inc(scores_made, 1)

                    def turn(b, k):
                        for a in range(2):
                            pe.wait_ge(probs_made, b * 32 + (2 * k + a + 1))
                            if not (isinstance(b, int) and b * STEPS + k == 0):
                                pe.wait_ge(ptlo_made, b * 32 + (2 * k + a - 1))
                            for m in range(T):
                                last = pe.transpose(t_bank[a][:, m * P:(m + 1) * P],
                                                    probs[:, k % 2, a, m * P:(m + 1) * P], ident[:])
                            last.then_inc(probs_turned, 1)

                    def attend_v(b, p):
                        for a in range(2):
                            pe.wait_ge(ptlo_made, b * 32 + (8 * p + 7 + a))
                            if a == 0:
                                if p == 0:
                                    pe.wait_ge(qkvlo_made, b * 12 + 12)
                                if not (isinstance(b, int) and b * PAIRS + p == 0):
                                    pe.wait_ge(ot_summed, b * 8 + 2 * p)
                            for m in range(T):
                                w = v[:, m, 2 * p + a, :, :].rearrange("p s d -> p (s d)")
                                pe.matmul(o_bank[a][:], w, pt_hi[:, a, m, :], start=m == 0, stop=False)
                                last = pe.matmul(o_bank[a][:], w, pt_lo[:, a, m, :], start=False, stop=m == T - 1)
                            last.then_inc(pv_done, 1)

                    def qk_matmuls(b, first, count, begin=False):
                        for g in range(first, first + count):
                            i, (m, s) = g // 12, divmod(g % 12, 3)
                            if g == 0:
                                pe.wait_ge(xt_loaded, b * 32 + 32)
                            if g % 12 == 0:
                                if i >= 2:
                                    pe.wait_ge(qkvlo_made, b * 12 + (i - 1))
                                elif not begin and isinstance(b, int) and b == 1:
                                    pe.wait_ge(qkvlo_made, 11 + i)
                                elif not begin:
                                    pe.wait_ge(o_made, b * 4 + (i - 5))
                            pair, w = i // 2, i % 2
                            a, c = ((w_hi, xt_hi), (w_hi, xt_lo), (w_lo, xt_hi))[s]
                            last = pe.matmul(g_bank[i % 2][:], a[:, w, m, pair * P:(pair + 1) * P], c[:, m, :],
                                             start=g % 12 == 0, stop=g % 12 == 11)
                            if g % 12 == 11:
                                last.then_inc(qkv_done, 1)

                    def v_unit(b, n):
                        pe.wait_ge(qkvlo_made, b * 12 + (7 + n))
                        for m in range(T):
                            for s, (a, c) in enumerate(((xt_hi, w_hi), (xt_hi, w_lo), (xt_lo, w_hi))):
                                last = pe.matmul(g_bank[n % 2][:], a[:, m, n * P:(n + 1) * P], c[:, 2, m, :],
                                                 start=m == 0 and s == 0, stop=m == 3 and s == 2)
                        last.then_inc(qkv_done, 1)

                    def project(b, n):
                        if n < 2:
                            if isinstance(b, int) and b == B:
                                pe.wait_ge(o_made, 4 * (B - 1) + n - 1)
                            else:
                                pe.wait_ge(qkvlo_made, b * 12 + (11 + n))
                        else:
                            pe.wait_ge(o_made, b * 4 + (n - 5))
                        for p in range(PAIRS):
                            if n == 0 and p == PAIRS - 1:
                                pe.wait_ge(otlo_made, b * 4)
                            for s, (a, c) in enumerate(((ot_hi, w_hi), (ot_hi, w_lo), (ot_lo, w_hi))):
                                last = pe.matmul(g_bank[n % 2][:], a[:, p, n * P:(n + 1) * P], c[:, 3, p, :],
                                                 start=p == 0 and s == 0, stop=p == 3 and s == 2)
                        last.then_inc(proj_done, 1)

                    def batch(b, last_part=True, more=True):
                        for k in range(STEPS):
                            turn(b, k)
                            if k + 2 < STEPS or more:
                                scores(b, k + 2)
                            if k < T and last_part:
                                project(b, k)
                            if k >= T and more:
                                qk_matmuls(b + 1, 8 * (k - T), 8)
                            if k % T == T - 1:
                                attend_v(b, k // T)
                        if more:
                            for n in range(T):
                                v_unit(b + 1, n)

                    qk_matmuls(0, 0, 96, begin=True)
                    for n in range(T):
                        v_unit(0, n)
                    scores(0, 0)
                    scores(0, 1)
                    batch(0, last_part=False)
                    with pe.Fori(1, B - 1, 1) as b:
                        batch(b)
                    batch(B - 1, more=False)
                    for n in range(T):
                        project(B, n)

                @block.scalar
                def _(act):
                    def exponent(b, k):
                        for a in range(2):
                            act.wait_ge(max_found, b * 32 + (2 * k + a + 1))
                            act.activation(probs[:, k % 2, a, :], probs[:, k % 2, a, :], ACT.Exp,
                                           bias=bias_row[:, k % 4, a:a + 1], scale=-1.0,
                                           accum_out=sums[:, k % 4, a:a + 1]).then_inc(exp_made, 1)

                    def pt_hi_part(b, k):
                        n = k % T
                        for a in range(2):
                            act.wait_ge(probs_turned, b * 32 + (2 * k + a + 1))
                            act.activation(pt_hi[:, a, :, n * P:(n + 1) * P],
                                           t_bank[a][:].rearrange("p (m n) -> p m n", m=T), ACT.Copy)\
                                .then_inc(pthi_made, 1)

                    def qk_hi_part(b, i):
                        act.wait_ge(qkv_done, b * 12 + (i + 1))
                        act.activation((q_hi, k_hi)[i % 2][:, i // 2, :], g_bank[i % 2][:], ACT.Copy)\
                            .then_inc(qkvhi_made, 1)

                    def v_hi_part(b, n):
                        act.wait_ge(qkv_done, b * 12 + (n + 9))
                        act.activation(v[:, n, :, 0, :], g_bank[n % 2][:].rearrange("p (h d) -> p h d", d=HEAD),
                                       ACT.Copy).then_inc(qkvhi_made, 1)

                    def ot_parts(b, p):
                        act.wait_ge(pv_done, b * 8 + (2 * p + 1))
                        if not (isinstance(b, int) and b * PAIRS + p == 0):
                            act.wait_ge(otlo_made, b * 4 + p)
                        act.activation(ot[0:HEAD, :], o_bank[0][HEAD:P, :], ACT.Copy).then_inc(ot_half, 1)
                        act.wait_ge(pv_done, b * 8 + (2 * p + 2))
                        act.activation(ot[HEAD:P, :], o_bank[1][0:HEAD, :], ACT.Copy).then_inc(ot_half, 1)
                        act.wait_ge(ot_summed, b * 8 + (2 * p + 2))
                        act.activation(ot_hi[:, p, :], ot[:], ACT.Copy).then_inc(othi_made, 1)

                    def layernorm(b, n):
                        act.wait_ge(shift_made[0], b * 4 + (n - 3))
                        if not (isinstance(b, int) and b == 1 and n == 0):
                            act.wait_ge(y_made, b * 4 + (n - 4))
                        act.activation(t[:], o[:, n, :], ACT.Identity, bias=shift[:, n, 0:1],
                                       scale=rstd[:, n, 0:1]).then_inc(ln_made, 1)

                    def result(b, n):
                        act.wait_ge(shift_made[1], b * 4 + (n - 3))
                        act.activation(o[:, n, :], t[:], ACT.Identity, bias=shift[:, n, 1:2],
                                       scale=rstd[:, n, 1:2]).then_inc(y_made, 1)

                    def batch(b, attend=True, last_part=True, more=True):
                        for k in range(STEPS):
                            if attend:
                                pt_hi_part(b, k)
                                if k + 2 < STEPS or more:
                                    exponent(b, k + 2)
                            if last_part:
                                if k - 3 in ln_step:
                                    result(b, ln_step[k - 3])
                                if k in ln_step:
                                    layernorm(b, ln_step[k])
                            if attend and more and k in unit_step:
                                qk_hi_part(b + 1, unit_step.index(k))
                            if attend and k % T == 0 and k > 0:
                                ot_parts(b, k // T - 1)
                        if attend:
                            ot_parts(b, PAIRS - 1)
                        if attend and more:
                            for n in range(T):
                                v_hi_part(b + 1, n)

                    for i in range(QK):
                        qk_hi_part(0, i)
                    for n in range(T):
                        v_hi_part(0, n)
                    exponent(0, 0)
                    exponent(0, 1)
                    batch(0, last_part=False)
                    batch(1)
                    with act.Fori(2, B - 1, 1) as b:
                        batch(b)
                    batch(B - 1, more=False)
                    batch(B, attend=False)

                @block.vector
                def _(dve):
                    def masked_max(b, k, waited=False):
                        if not waited:
                            dve.wait_ge(scores_made, b * 32 + (2 * k + 2))
                        for a in range(2):
                            dve.tensor_tensor_reduce(probs[:, k % 2, a, :], s_bank[a][:], mask_bias[:, k % T, :],
                                                     -SCALE, 3.0e38, ALU.add, ALU.min,
                                                     bias_row[:, k % 4, a:a + 1]).then_inc(max_found, 1)

                    def inverse(b, k):
                        dve.wait_ge(exp_made, b * 32 + (2 * k + 2))
                        dve.reciprocal(inv_sums[:, k % 4, :], sums[:, k % 4, :]).then_inc(inv_made, 1)

                    def pt_lo_part(b, k, scores_too):
                        cols = slice(k % T * P, (k % T + 1) * P)
                        for a in range(2):
                            dve.wait_ge(pthi_made, b * 32 + (2 * k + a + 1))
                            if a == 1 and scores_too:
                                dve.wait_ge(scores_made, b * 32 + (2 * k + 6))
                            dve.tensor_tensor(pt_lo[:, a, :, cols], t_bank[a][:].rearrange("p (m n) -> p m n", m=T),
                                              f32(pt_hi[:, a, :, cols]), ALU.subtract).then_inc(ptlo_made, 1)

                    def qk_lo_part(b, i):
                        dve.wait_ge(qkvhi_made, b * 12 + (i + 1))
                        hi, lo = ((q_hi, q_lo), (k_hi, k_lo))[i % 2]
                        dve.tensor_tensor(lo[:, i // 2, :], g_bank[i % 2][:], f32(hi[:, i // 2, :]), ALU.subtract)\
                            .then_inc(qkvlo_made, 1)

                    def v_lo_part(b, n):
                        dve.wait_ge(qkvhi_made, b * 12 + (n + 9))
                        dve.tensor_tensor(v[:, n, :, 1, :], g_bank[n % 2][:].rearrange("p (h d) -> p h d", d=HEAD),
                                          f32(v[:, n, :, 0, :]), ALU.subtract).then_inc(qkvlo_made, 1)

                    def ot_parts(b, p):
                        for a in range(2):
                            dve.wait_ge(ot_half, b * 8 + (2 * p + a + 1))
                            h = slice(a * HEAD, (a + 1) * HEAD)
                            dve.tensor_tensor(ot[h, :], o_bank[a][h, :], ot[h, :], ALU.add).then_inc(ot_summed, 1)
                        dve.wait_ge(othi_made, b * 4 + (p + 1))
                        dve.tensor_tensor(ot_lo[:, p, :], ot[:], f32(ot_hi[:, p, :]), ALU.subtract)\
                            .then_inc(otlo_made, 1)

                    def statistics(b, n, i, rows_of):
                        dve.bn_stats(stats[:, n, i, :], rows_of).then_inc(stats_made[i], 1)
                        dve.wait_ge(stats_made[i], 1)
                        dve.wait_ge(stats_made[i], b * 4 + (n - 3))
                        dve.bn_aggr(mean_var[:, n, i, :], stats[:, n, i, :]).then_inc(mean_made[i], 1)
                        dve.wait_ge(mean_made[i], b * 4 + (n - 3))
                        dve.tensor_scalar(var_eps[:, n, i:i + 1], mean_var[:, n, i, 1:2], EPS, None, ALU.add)\
                            .then_inc(eps_added[i], 1)

                    def row_shift(b, n, i):
                        dve.wait_ge(rstd_made[i], b * 4 + (n - 3))
                        dve.tensor_scalar(shift[:, n, i:i + 1], mean_var[:, n, i, 0:1], rstd[:, n, i:i + 1], -1.0,
                                          ALU.mult, ALU.mult).then_inc(shift_made[i], 1)

                    def add_bproj(b, n):
                        dve.wait_ge(proj_done, b * 4 + (n - 3))
                        if not (isinstance(b, int) and b == 1):
                            dve.wait_ge(y_stored, b * 64 + 16 * (n - 7))
                        dve.tensor_tensor(o[:, n, :], g_bank[n % 2][:], bproj_row[:], ALU.add).then_inc(o_made, 1)
                        dve.wait_ge(o_made, b * 4 + (n - 3))
                        statistics(b, n, 0, o[:, n, :])

                    def add_beta_o(b, n):
                        dve.wait_ge(gamma_done, b * 4 + (n - 3))
                        dve.tensor_tensor(t[:], t[:], beta_row[:], ALU.add).then_inc(beta_done, 1)
                        dve.wait_ge(beta_done, b * 4 + (n - 3))
                        dve.tensor_tensor(t[:], t[:], o[:, n, :], ALU.add).then_inc(o_added, 1)

                    def add_u(b, n):
                        dve.wait_ge(o_added, b * 4 + (n - 3))
                        dve.wait_ge(u_loaded, b * 64 + 16 * (n - 3))
                        dve.tensor_tensor(t[:], t[:], o[:, n, :], ALU.add).then_inc(u_added, 1)
                        dve.wait_ge(u_added, b * 4 + (n - 3))
                        statistics(b, n, 1, t[:])

                    def batch(b, attend=True, last_part=True, more=True):
                        for k in range(STEPS):
                            if last_part:
                                if 1 <= k <= T:
                                    row_shift(b, k - 1, 0)
                                if k - 3 in ln_step:
                                    row_shift(b, ln_step[k - 3], 1)
                            if attend:
                                if k + 1 < STEPS or more:
                                    inverse(b, k + 1)
                                ahead = k + 2 < STEPS or more
                                pt_lo_part(b, k, ahead)
                                if ahead:
                                    masked_max(b, k + 2, waited=True)
                            if last_part:
                                if k < T:
                                    add_bproj(b, k)
                                if k - 1 in ln_step:
                                    add_beta_o(b, ln_step[k - 1])
                                if k - 2 in ln_step:
                                    add_u(b, ln_step[k - 2])
                            if attend and more and k in unit_step:
                                qk_lo_part(b + 1, unit_step.index(k))
                            if attend and k % T == 0 and k > 0:
                                ot_parts(b, k // T - 1)
                        if attend:
                            ot_parts(b, PAIRS - 1)
                        if attend and more:
                            for n in range(T):
                                v_lo_part(b + 1, n)

                    for i in range(QK):
                        qk_lo_part(0, i)
                    for n in range(T):
                        v_lo_part(0, n)
                    masked_max(0, 0)
                    masked_max(0, 1)
                    inverse(0, 0)
                    batch(0, last_part=False)
                    batch(1)
                    with dve.Fori(2, B - 1, 1) as b:
                        batch(b)
                    batch(B - 1, more=False)
                    batch(B, attend=False)


_INS = ["x", "adj", "L0_gnn_weight", "L0_gnn_bias", "L1_gnn_w_qkv", "L1_gnn_w_proj", "L1_gnn_b_proj",
        "L1_gnn_ln_gamma", "L1_gnn_ln_beta"]


def kernel(**inputs):
    import numpy as _np
    import concourse.bacc as _bacc
    from concourse import mybir as _mybir
    from concourse.bass_utils import run_bass_kernel_spmd as _run

    nc = _bacc.Bacc("TRN2", target_bir_lowering=False, num_devices=1)
    arrays, args = {}, []
    for name in _INS:
        a = _np.ascontiguousarray(inputs[name])
        arrays[f"in_{name}_dram"] = a
        args.append(nc.dram_tensor(f"in_{name}_dram", a.shape, _mybir.dt.from_np(a.dtype), kind="ExternalInput").ap())
    shape = arrays["in_x_dram"].shape
    out = nc.dram_tensor("out_0_dram", shape, _mybir.dt.float32, kind="ExternalOutput").ap()
    graph_layers(nc, *args, out)
    r = _run(nc, [arrays], core_ids=[0])
    return r.results[0]["out_0_dram"]
```

```python
from contextlib import ExitStack

import concourse.bass as bass
from concourse import mybir

F32 = mybir.dt.float32
F32R = mybir.dt.float32r
BF16 = mybir.dt.bfloat16
ALU = mybir.AluOpType
ACT = mybir.ActivationFunctionType
P = 128
EPS = 1e-5
MASKED = -1.0e30


def graph_layers(nc, x, adj, w0, b0, wqkv, wproj, bproj, gamma, beta, out):
    B, N, D = x.shape
    T = N // P
    HEAD = 64
    PAIRS = D // (2 * HEAD)
    SCALE = float(HEAD) ** -0.5
    assert N == 512 and D == 512 and T == 4 and PAIRS == 4

    u_dram = nc.dram_tensor("u_rows", [B, N, D], F32, kind="Internal").ap()
    uth_dram = nc.dram_tensor("ut_hi", [B, T, P, T, P], F32, kind="Internal").ap()
    utl_dram = nc.dram_tensor("ut_lo", [B, T, P, T, P], F32, kind="Internal").ap()

    def rows(m):
        return m.rearrange("(t p) d -> p t d", p=P)

    def f32(ap):
        return ap.bitcast(F32)

    with ExitStack() as whole:
        def keep(name, shape, dt):
            return whole.enter_context(nc.sbuf_tensor(name, shape, dt))

        w_hi = keep("w_hi", [P, 4, T, D], F32R)
        w_lo = keep("w_lo", [P, 4, T, D], F32R)
        mask_bias = keep("mask_bias", [P, T, N], BF16)
        ident = keep("ident", [P, P], F32)
        half_neg = keep("half_neg", [P, 1], F32)
        bproj_row = keep("bproj_row", [P, D], F32)
        gamma_row = keep("gamma_row", [P, D], F32)
        beta_row = keep("beta_row", [P, D], F32)

        psum = [whole.enter_context(nc.psum_tensor(f"bank{i}", [P, 512], F32)) for i in range(8)]

        with ExitStack() as first:
            def sb(name, shape, dt):
                return first.enter_context(nc.sbuf_tensor(name, shape, dt))

            def sem(name):
                return first.enter_context(nc.semaphore(name))

            adjt_hi = sb("adjt_hi", [P, T, N], F32R)
            adjt_lo = sb("adjt_lo", [P, T, N], F32R)
            w0_hi = sb("w0_hi", [P, T, D], F32R)
            w0_lo = sb("w0_lo", [P, T, D], F32R)
            b0_row = sb("b0_row", [P, 1, D], F32)
            x_in = sb("x_in", [P, T, D], F32)
            xb = sb("xb", [P, T, D], F32)
            x_hi = sb("x_hi", [P, T, D], F32R)
            x_lo = sb("x_lo", [P, T, D], F32R)
            yt_hi = sb("yt_hi", [P, T, N], F32R)
            yt_lo = sb("yt_lo", [P, T, N], F32R)
            res = sb("res", [P, 2, D], F32)
            u = sb("u", [P, T, D], F32)
            ut_hi = sb("ut_hi_sb", [P, T, N], F32R)
            ut_lo = sb("ut_lo_sb", [P, T, N], F32R)
            stats = sb("stats", [P, T, 6], F32)
            mean_var = sb("mean_var", [P, T, 2], F32)
            var_eps = sb("var_eps", [P, T], F32)
            rstd = sb("rstd", [P, T], F32)
            shift = sb("shift", [P, T], F32)

            stage = [x_in, xb, u]
            ident_made = sem("ident_made")
            rows_in = sem("rows_in")
            chunk_in = [sem(f"chunk_in{i}") for i in range(3)]
            hi_made = sem("hi_made")
            lo_made = sem("lo_made")
            adj_turned = sem("adj_turned")
            adjt_hi_made = sem("adjt_hi_made")
            adjt_lo_made = sem("adjt_lo_made")
            mask_made = sem("mask_made")

            sources = [rows(adj), rows(w0)] + [rows(wqkv[:, i * D:(i + 1) * D]) for i in range(3)] + [rows(wproj)]
            parts = [None, (w0_hi[:], w0_lo[:])] + [(w_hi[:, i], w_lo[:, i]) for i in range(4)]

            with nc.Block() as block:
                @block.sync
                def _(sp):
                    for c in range(6):
                        if c == 3:
                            sp.wait_ge(adj_turned, T)
                            sp.wait_ge(mask_made, 1)
                        elif c > 3:
                            sp.wait_ge(lo_made, c - 3)
                        sp.dma_start(stage[c % 3][:], sources[c]).then_inc(chunk_in[c % 3], 16)
                    for row, src in ((b0_row[:, 0, :], b0), (bproj_row[:], bproj), (gamma_row[:], gamma),
                                     (beta_row[:], beta)):
                        sp.dma_start(row, src.partition_broadcast(P)).then_inc(rows_in, 16)
                    sp.wait_ge(rows_in, 64)

                @block.gpsimd
                def _(pool):
                    pool.memset(half_neg[:], -0.5)
                    pool.memset(ident[:], 0.0).then_inc(ident_made, 1)
                    pool.wait_ge(ident_made, 1)
                    pool.affine_select(out=ident[:], in_=ident[:], compare_op=ALU.not_equal, fill=1.0, base=0,
                                       pattern=[[-1, P]], channel_multiplier=1).then_inc(ident_made, 1)

                @block.tensor
                def _(pe):
                    pe.wait_ge(ident_made, 2)
                    pe.wait_ge(chunk_in[0], 16)
                    for m in range(T):
                        for n in range(T):
                            last = pe.transpose(psum[m][:, n * P:(n + 1) * P], stage[0][:, n, m * P:(m + 1) * P],
                                                ident[:])
                        last.then_inc(adj_turned, 1)

                @block.scalar
                def _(act):
                    for m in range(T):
                        act.wait_ge(adj_turned, m + 1)
                        act.activation(adjt_hi[:, m, :], psum[m][:], ACT.Copy).then_inc(adjt_hi_made, 1)
                    for c in range(1, 6):
                        act.wait_ge(chunk_in[c % 3], 16 * (c // 3 + 1))
                        act.activation(parts[c][0], stage[c % 3][:], ACT.Copy).then_inc(hi_made, 1)

                @block.vector
                def _(dve):
                    dve.wait_ge(chunk_in[0], 16)
                    dve.tensor_scalar(mask_bias[:], stage[0][:], 0.0, MASKED, ALU.is_equal, ALU.mult)\
                        .then_inc(mask_made, 1)
                    for m in range(T):
                        dve.wait_ge(adjt_hi_made, m + 1)
                        dve.tensor_tensor(adjt_lo[:, m, :], psum[m][:], f32(adjt_hi[:, m, :]), ALU.subtract)\
                            .then_inc(adjt_lo_made, 1)
                    for c in range(1, 6):
                        dve.wait_ge(hi_made, c)
                        dve.tensor_tensor(parts[c][1], stage[c % 3][:], f32(parts[c][0]), ALU.subtract)\
                            .then_inc(lo_made, 1)

            x_loaded = sem("x_loaded")
            xhi_made = sem("xhi_made")
            xlo_made = sem("xlo_made")
            xb_made = sem("xb_made")
            yz_done = sem("yz_done")
            yhi_made = sem("yhi_made")
            ylo_made = sem("ylo_made")
            res_made = sem("res_made")
            stats_made = sem("stats_made")
            mean_made = sem("mean_made")
            eps_added = sem("eps_added")
            rstd_made = sem("rstd_made")
            shift_made = sem("shift_made")
            u_made = sem("u_made")
            u_turned = sem("u_turned")
            uthi_made = sem("uthi_made")
            utlo_made = sem("utlo_made")
            u_stored = sem("u_stored")
            ut_stored = [sem(f"ut_stored{j}") for j in range(T)]

            yz_bank = psum[0:4]
            turn_bank = psum[4:6]

            with nc.Block() as block:
                @block.sync
                def _(sp):
                    def store_ut(b, j):
                        cols = slice(j * P, (j + 1) * P)
                        sp.wait_ge(utlo_made, b * 4 + (j + 1))
                        sp.dma_start(uth_dram[b, j], f32(ut_hi[:, :, cols])).then_inc(ut_stored[j], 16)
                        sp.dma_start(utl_dram[b, j], f32(ut_lo[:, :, cols])).then_inc(ut_stored[j], 16)

                    def store_u(b):
                        sp.wait_ge(u_made, b * 4 + 4)
                        sp.dma_start(rows(u_dram[b]), u[:]).then_inc(u_stored, 16)

                    def load_x(b):
                        sp.wait_ge(xb_made, b)
                        sp.dma_start(x_in[:], rows(x[b])).then_inc(x_loaded, 16)

                    def batch(b, first=False, last=False):
                        if not last:
                            load_x(b + 1)
                        if not first:
                            store_ut(b - 1, 2)
                            store_ut(b - 1, 3)
                        store_ut(b, 0)
                        store_u(b)
                        store_ut(b, 1)

                    sp.dma_start(x_in[:], rows(x[0])).then_inc(x_loaded, 16)
                    batch(0, first=True)
                    with sp.Fori(1, B - 1, 1) as b:
                        batch(b)
                    batch(B - 1, last=True)
                    store_ut(B - 1, 2)
                    store_ut(B - 1, 3)
                    sp.wait_ge(u_stored, 16 * B)
                    for j in range(T):
                        sp.wait_ge(ut_stored[j], 32 * B)

                @block.gpsimd
                def _(pool):
                    def batch(b, first=False):
                        pool.wait_ge(xlo_made, b * 4 + 4)
                        if not first:
                            pool.wait_ge(res_made, b * 4)
                        pool.tensor_tensor(xb[:], x_in[:], b0_row[:].to_broadcast((P, T, D)), ALU.add)\
                            .then_inc(xb_made, 1)
                        for j in range(T):
                            pool.wait_ge(eps_added, b * 4 + (j + 1))
                            pool.tensor_tensor(rstd[:, j:j + 1], var_eps[:, j:j + 1], half_neg[:], ALU.pow)\
                                .then_inc(rstd_made, 1)

                    batch(0, first=True)
                    with pool.Fori(1, B, 1) as b:
                        batch(b)

                @block.tensor
                def _(pe):
                    def y(b, j, first=False):
                        bank = yz_bank[j]
                        if not first:
                            pe.wait_ge(res_made, b * 4 + (j - 3))
                        n = 0
                        for a, c in ((x_hi, adjt_hi), (x_hi, adjt_lo), (x_lo, adjt_hi)):
                            if j == 0 and c is adjt_hi:
                                pe.wait_ge(xhi_made if a is x_hi else xlo_made, b * 4 + 4)
                            for m in range(T):
                                last = pe.matmul(bank[:], a[:, m, j * P:(j + 1) * P], c[:, m, :],
                                                 start=n == 0, stop=n == 11)
                                n += 1
                        last.then_inc(yz_done, 1)

                    def z(b, j):
                        bank = yz_bank[j]
                        for m in range(T):
                            if j == 0:
                                pe.wait_ge(ylo_made, b * 4 + (m + 1))
                            for i, (a, c) in enumerate(((yt_hi, w0_hi), (yt_hi, w0_lo), (yt_lo, w0_hi))):
                                last = pe.matmul(bank[:], a[:, m, j * P:(j + 1) * P], c[:, m, :],
                                                 start=m == 0 and i == 0, stop=m == 3 and i == 2)
                        last.then_inc(yz_done, 1)

                    def turn(b, j, free=True):
                        pe.wait_ge(u_made, b * 4 + (j + 1))
                        if free:
                            pe.wait_ge(utlo_made, b * 4 + (j - 1))
                        for d in range(T):
                            last = pe.transpose(turn_bank[j % 2][:, d * P:(d + 1) * P], u[:, j, d * P:(d + 1) * P],
                                                ident[:])
                        last.then_inc(u_turned, 1)

                    def batch(b, first=False):
                        y(b, 0, first)
                        if not first:
                            turn(b - 1, 2)
                        y(b, 1, first)
                        if not first:
                            turn(b - 1, 3)
                        y(b, 2, first)
                        y(b, 3, first)
                        z(b, 0)
                        z(b, 1)
                        z(b, 2)
                        turn(b, 0, free=not first)
                        z(b, 3)
                        turn(b, 1, free=not first)

                    batch(0, first=True)
                    with pe.Fori(1, B, 1) as b:
                        batch(b)
                    turn(B - 1, 2)
                    turn(B - 1, 3)

                @block.scalar
                def _(act):
                    def x_hi_part(b):
                        act.wait_ge(x_loaded, b * 16 + 16)
                        for m in range(T):
                            act.activation(x_hi[:, m, :], x_in[:, m, :], ACT.Copy).then_inc(xhi_made, 1)

                    def y_hi_part(b, j):
                        act.wait_ge(yz_done, b * 8 + (j + 1))
                        act.activation(yt_hi[:, j, :], yz_bank[j][:], ACT.Copy).then_inc(yhi_made, 1)

                    def normalise(b, j):
                        act.wait_ge(shift_made, b * 4 + (j + 1))
                        act.activation(u[:, j, :], res[:, j % 2, :], ACT.Identity, bias=shift[:, j:j + 1],
                                       scale=rstd[:, j:j + 1]).then_inc(u_made, 1)

                    def ut_hi_part(b, j):
                        act.wait_ge(u_turned, b * 4 + (j + 1))
                        if not (isinstance(b, int) and b == 0):
                            act.wait_ge(ut_stored[j], b * 32)
                        act.activation(ut_hi[:, :, j * P:(j + 1) * P],
                                       turn_bank[j % 2][:].rearrange("p (d n) -> p d n", d=T), ACT.Copy)\
                            .then_inc(uthi_made, 1)

                    def batch(b, first=False, last=False):
                        for j in range(T):
                            y_hi_part(b, j)
                            if not first and j < 2:
                                ut_hi_part(b - 1, j + 2)
                        if not last:
                            x_hi_part(b + 1)
                        if not first:
                            act.wait_ge(u_stored, b * 16)
                            act.wait_ge(u_turned, b * 4)
                        normalise(b, 0)
                        normalise(b, 1)
                        ut_hi_part(b, 0)
                        normalise(b, 2)
                        ut_hi_part(b, 1)
                        normalise(b, 3)

                    x_hi_part(0)
                    batch(0, first=True)
                    batch(1)
                    with act.Fori(2, B - 1, 1) as b:
                        batch(b)
                    batch(B - 1, last=True)
                    ut_hi_part(B - 1, 2)
                    ut_hi_part(B - 1, 3)

                @block.vector
                def _(dve):
                    def x_lo_part(b, m):
                        dve.wait_ge(xhi_made, b * 4 + (m + 1))
                        dve.tensor_tensor(x_lo[:, m, :], x_in[:, m, :], f32(x_hi[:, m, :]), ALU.subtract)\
                            .then_inc(xlo_made, 1)

                    def y_lo_part(b, j):
                        dve.wait_ge(yhi_made, b * 4 + (j + 1))
                        dve.tensor_tensor(yt_lo[:, j, :], yz_bank[j][:], f32(yt_hi[:, j, :]), ALU.subtract)\
                            .then_inc(ylo_made, 1)

                    def row_stats(b, j, free=True):
                        dve.wait_ge(yz_done, b * 8 + (j + 5))
                        if j == 0:
                            dve.wait_ge(xb_made, b + 1)
                        if free:
                            dve.wait_ge(u_made, b * 4 + (j - 1))
                        dve.tensor_tensor(res[:, j % 2, :], yz_bank[j][:], xb[:, j, :], ALU.add)\
                            .then_inc(res_made, 1)
                        dve.wait_ge(res_made, b * 4 + (j + 1))
                        dve.bn_stats(stats[:, j, :], res[:, j % 2, :]).then_inc(stats_made, 1)
                        dve.wait_ge(stats_made, 1)
                        dve.wait_ge(stats_made, b * 4 + (j + 1))
                        dve.bn_aggr(mean_var[:, j, :], stats[:, j, :]).then_inc(mean_made, 1)
                        dve.wait_ge(mean_made, b * 4 + (j + 1))
                        dve.tensor_scalar(var_eps[:, j:j + 1], mean_var[:, j, 1:2], EPS, None, ALU.add)\
                            .then_inc(eps_added, 1)

                    def row_shift(b, j):
                        dve.wait_ge(rstd_made, b * 4 + (j + 1))
                        dve.tensor_scalar(shift[:, j:j + 1], mean_var[:, j, 0:1], rstd[:, j:j + 1], -1.0,
                                          ALU.mult, ALU.mult).then_inc(shift_made, 1)

                    def ut_lo_part(b, j):
                        dve.wait_ge(uthi_made, b * 4 + (j + 1))
                        cols = slice(j * P, (j + 1) * P)
                        dve.tensor_tensor(ut_lo[:, :, cols], turn_bank[j % 2][:].rearrange("p (d n) -> p d n", d=T),
                                          f32(ut_hi[:, :, cols]), ALU.subtract).then_inc(utlo_made, 1)

                    def batch(b, first=False, last=False):
                        for j in range(T):
                            y_lo_part(b, j)
                            if not first and j < 2:
                                ut_lo_part(b - 1, j + 2)
                        if not last:
                            x_lo_part(b + 1, 0)
                            x_lo_part(b + 1, 1)
                        row_stats(b, 0, free=not first)
                        if not last:
                            x_lo_part(b + 1, 2)
                        row_shift(b, 0)
                        row_stats(b, 1, free=not first)
                        if not last:
                            x_lo_part(b + 1, 3)
                        row_shift(b, 1)
                        row_stats(b, 2)
                        ut_lo_part(b, 0)
                        row_shift(b, 2)
                        row_stats(b, 3)
                        ut_lo_part(b, 1)
                        row_shift(b, 3)

                    for m in range(T):
                        x_lo_part(0, m)
                    batch(0, first=True)
                    with dve.Fori(1, B - 1, 1) as b:
                        batch(b)
                    batch(B - 1, last=True)
                    ut_lo_part(B - 1, 2)
                    ut_lo_part(B - 1, 3)

        with ExitStack() as second:
            def sb(name, shape, dt):
                return second.enter_context(nc.sbuf_tensor(name, shape, dt))

            def sem(name):
                return second.enter_context(nc.semaphore(name))

            xt_hi = sb("xt_hi", [P, T, N], F32R)
            xt_lo = sb("xt_lo", [P, T, N], F32R)
            q_hi = sb("q_hi", [P, PAIRS, N], F32R)
            q_lo = sb("q_lo", [P, PAIRS, N], F32R)
            k_hi = sb("k_hi", [P, PAIRS, N], F32R)
            k_lo = sb("k_lo", [P, PAIRS, N], F32R)
            v = sb("v", [P, T, 2 * PAIRS, 2, HEAD], F32R)
            probs = sb("probs", [P, 2, 2, N], F32)
            pt_hi = sb("pt_hi", [P, 2, T, N], F32R)
            pt_lo = sb("pt_lo", [P, 2, T, N], F32R)
            ot_hi = sb("ot_hi", [P, PAIRS, N], F32R)
            ot_lo = sb("ot_lo", [P, PAIRS, N], F32R)
            ot = sb("ot", [P, N], F32)
            o = sb("o", [P, T, D], F32)
            t = sb("t", [P, D], F32)
            bias_row = sb("bias_row", [P, 4, 2], F32)
            sums = sb("sums", [P, 4, 2], F32)
            inv_sums = sb("inv_sums", [P, 4, 2], F32)
            stats = sb("o_stats", [P, T, 2, 6], F32)
            mean_var = sb("o_mean_var", [P, T, 2, 2], F32)
            var_eps = sb("o_var_eps", [P, T, 2], F32)
            rstd = sb("o_rstd", [P, T, 2], F32)
            shift = sb("o_shift", [P, T], F32)

            s_bank, t_bank, o_bank, g_bank = psum[0:2], psum[2:4], psum[4:6], psum[6:8]

            STEPS = PAIRS * T
            STRIP = 32
            scores_made = sem("scores_made")
            max_found = sem("max_found")
            exp_made = sem("exp_made")
            inv_made = sem("inv_made")
            probs_made = sem("probs_made")
            probs_turned = sem("probs_turned")
            pthi_made = sem("pthi_made")
            ptlo_made = sem("ptlo_made")
            pv_done = sem("pv_done")
            ot_half = sem("ot_half")
            ot_summed = sem("ot_summed")
            othi_made = sem("othi_made")
            otlo_made = sem("otlo_made")
            xt_loaded = sem("xt_loaded")
            qkv_done = sem("qkv_done")
            qkvhi_made = sem("qkvhi_made")
            qkvlo_made = sem("qkvlo_made")
            proj_done = sem("proj_done")
            o_made = sem("o_made")
            stats_made = [sem(f"o_stats_made{i}") for i in range(2)]
            mean_made = [sem(f"o_mean_made{i}") for i in range(2)]
            eps_added = [sem(f"o_eps_added{i}") for i in range(2)]
            rstd_made = [sem(f"o_rstd_made{i}") for i in range(2)]
            shift_made = sem("o_shift_made")
            gamma_done = sem("gamma_done")
            o_added = sem("o_added")
            u_loaded = sem("u_loaded")
            beta_done = sem("beta_done")
            u_added = sem("u_added")
            y_made = sem("y_made")
            y_stored = sem("y_stored")

            QK = 2 * PAIRS
            unit_step = [4 + (12 * (i + 1) + 7) // 8 - 1 for i in range(QK)]
            LN_STEP = [4, 7, 11, 14]
            assert LN_STEP[-1] + 2 == STEPS

            def row_at(k):
                return LN_STEP.index(k) if k in LN_STEP else None

            with nc.Block() as block:
                @block.sync
                def _(sp):
                    def load_xt(b, first=False):
                        if not first:
                            sp.wait_ge(qkv_done, b * 12)
                        for j in range(T):
                            cols = slice(j * P, (j + 1) * P)
                            sp.dma_start(f32(xt_hi[:, :, cols]), uth_dram[b, j]).then_inc(xt_loaded, 16)
                            sp.dma_start(f32(xt_lo[:, :, cols]), utl_dram[b, j]).then_inc(xt_loaded, 16)

                    def finish(b):
                        for n in range(T):
                            sp.wait_ge(o_added, b * 4 + (n - 3))
                            sp.dma_start(o[:, n, :], u_dram[b - 1, n * P:(n + 1) * P, :]).then_inc(u_loaded, 16)
                            sp.wait_ge(y_made, b * 4 + (n - 3))
                            sp.dma_start(out[b - 1, n * P:(n + 1) * P, :], o[:, n, :]).then_inc(y_stored, 16)

                    load_xt(0, first=True)
                    load_xt(1)
                    with sp.Fori(1, B - 1, 1) as b:
                        load_xt(b + 1)
                        finish(b)
                    finish(B - 1)
                    finish(B)
                    sp.wait_ge(y_stored, 64 * B)

                @block.gpsimd
                def _(pool):
                    def normalise(b, k):
                        pool.wait_ge(inv_made, b * STEPS + (k + 1))
                        strip, rest = slice(0, STRIP), slice(STRIP, N)
                        pool.tensor_tensor(probs[:, k % 2, 0, strip], probs[:, k % 2, 0, strip],
                                           inv_sums[:, k % 4, 0:1].to_broadcast((P, STRIP)), ALU.mult)
                        for a, cols in ((0, rest), (1, slice(0, N))):
                            pool.tensor_scalar(probs[:, k % 2, a, cols], probs[:, k % 2, a, cols],
                                               inv_sums[:, k % 4, a:a + 1], 0.0, ALU.mult, ALU.add)\
                                .then_inc(probs_made, 1)

                    def power(b, n, i):
                        pool.wait_ge(eps_added[i], b * 4 + (n - 3))
                        pool.tensor_tensor(rstd[:, n, i:i + 1], var_eps[:, n, i:i + 1], half_neg[:], ALU.pow)\
                            .then_inc(rstd_made[i], 1)

                    def add_u_beta(b, n):
                        pool.wait_ge(u_loaded, b * 64 + 16 * (n - 3))
                        pool.tensor_tensor(o[:, n, :], o[:, n, :], beta_row[:], ALU.add).then_inc(beta_done, 1)
                        pool.wait_ge(o_added, b * 4 + (n - 3))
                        pool.wait_ge(beta_done, b * 4 + (n - 3))
                        pool.tensor_tensor(t[:], t[:], o[:, n, :], ALU.add).then_inc(u_added, 1)

                    def batch(b, attend=True, last_part=True, more=True):
                        for k in range(STEPS):
                            if attend and (k + 1 < STEPS or more):
                                normalise(b, k + 1)
                            if last_part and k < T:
                                power(b, k, 0)
                            if last_part and row_at(k - 1) is not None:
                                add_u_beta(b, row_at(k - 1))
                            if last_part and row_at(k - 2) is not None:
                                power(b, row_at(k - 2), 1)
                        if last_part:
                            power(b, T - 1, 1)

                    normalise(0, 0)
                    batch(0, last_part=False)
                    with pool.Fori(1, B - 1, 1) as b:
                        batch(b)
                    batch(B - 1, more=False)
                    batch(B, attend=False)

                @block.tensor
                def _(pe):
                    def scores(b, k):
                        pair, n = k // T % PAIRS, k % T
                        if n == 0:
                            pe.wait_ge(qkvlo_made, (b + k // STEPS) * 12 + (2 * pair + 2))
                        parts = ((q_hi, k_hi), (q_hi, k_lo), (q_lo, k_hi))
                        for a in range(2):
                            if not (isinstance(b, int) and b * STEPS + k == 0):
                                pe.wait_ge(max_found, b * 32 + (2 * k + a - 1))
                        for i, (l, r) in enumerate(parts):
                            for a in range(2):
                                h = slice(a * HEAD, (a + 1) * HEAD)
                                last = pe.matmul(s_bank[a][:], l[h, pair, n * P:(n + 1) * P], r[h, pair, :],
                                                 start=i == 0, stop=i == 2)
                                if i == 2:
                                    last.then_inc(scores_made, 1)

                    def turn(b, k):
                        for a in range(2):
                            pe.wait_ge(probs_made, b * 32 + (2 * k + a + 1))
                            if not (isinstance(b, int) and b * STEPS + k == 0):
                                pe.wait_ge(ptlo_made, b * 32 + (2 * k + a - 1))
                            for m in range(T):
                                last = pe.transpose(t_bank[a][:, m * P:(m + 1) * P],
                                                    probs[:, k % 2, a, m * P:(m + 1) * P], ident[:])
                            last.then_inc(probs_turned, 1)

                    def attend_v(b, p):
                        for a in range(2):
                            pe.wait_ge(ptlo_made, b * 32 + (8 * p + 7 + a))
                            if a == 0:
                                if p == 0:
                                    pe.wait_ge(qkvlo_made, b * 12 + 12)
                                if not (isinstance(b, int) and b * PAIRS + p == 0):
                                    pe.wait_ge(ot_summed, b * 8 + 2 * p)
                            for m in range(T):
                                w = v[:, m, 2 * p + a, :, :].rearrange("p s d -> p (s d)")
                                pe.matmul(o_bank[a][:], w, pt_hi[:, a, m, :], start=m == 0, stop=False)
                                last = pe.matmul(o_bank[a][:], w, pt_lo[:, a, m, :], start=False, stop=m == T - 1)
                            last.then_inc(pv_done, 1)

                    def qk_matmuls(b, first, count, begin=False):
                        for g in range(first, first + count):
                            i, (m, s) = g // 12, divmod(g % 12, 3)
                            if g == 0:
                                pe.wait_ge(xt_loaded, b * 128 + 128)
                            if g % 12 == 0:
                                if i >= 2:
                                    pe.wait_ge(qkvlo_made, b * 12 + (i - 1))
                                elif not begin and isinstance(b, int) and b == 1:
                                    pe.wait_ge(qkvlo_made, 11 + i)
                                elif not begin:
                                    pe.wait_ge(o_made, b * 4 + (i - 5))
                            pair, w = i // 2, i % 2
                            a, c = ((w_hi, xt_hi), (w_hi, xt_lo), (w_lo, xt_hi))[s]
                            last = pe.matmul(g_bank[i % 2][:], a[:, w, m, pair * P:(pair + 1) * P], c[:, m, :],
                                             start=g % 12 == 0, stop=g % 12 == 11)
                            if g % 12 == 11:
                                last.then_inc(qkv_done, 1)

                    def v_unit(b, n):
                        pe.wait_ge(qkvlo_made, b * 12 + (7 + n))
                        for m in range(T):
                            for s, (a, c) in enumerate(((xt_hi, w_hi), (xt_hi, w_lo), (xt_lo, w_hi))):
                                last = pe.matmul(g_bank[n % 2][:], a[:, m, n * P:(n + 1) * P], c[:, 2, m, :],
                                                 start=m == 0 and s == 0, stop=m == 3 and s == 2)
                        last.then_inc(qkv_done, 1)

                    def project(b, n):
                        if n < 2:
                            if isinstance(b, int) and b == B:
                                pe.wait_ge(o_made, 4 * (B - 1) + n - 1)
                            else:
                                pe.wait_ge(qkvlo_made, b * 12 + (11 + n))
                        else:
                            pe.wait_ge(o_made, b * 4 + (n - 5))
                        for p in range(PAIRS):
                            if n == 0 and p >= PAIRS - 2:
                                pe.wait_ge(otlo_made, b * 4 + (p - 3))
                            for s, (a, c) in enumerate(((ot_hi, w_hi), (ot_hi, w_lo), (ot_lo, w_hi))):
                                last = pe.matmul(g_bank[n % 2][:], a[:, p, n * P:(n + 1) * P], c[:, 3, p, :],
                                                 start=p == 0 and s == 0, stop=p == 3 and s == 2)
                        last.then_inc(proj_done, 1)

                    def batch(b, last_part=True, more=True):
                        for k in range(STEPS):
                            turn(b, k)
                            if k + 2 < STEPS or more:
                                scores(b, k + 2)
                            if k < T and last_part:
                                project(b, k)
                            if k >= T and more:
                                qk_matmuls(b + 1, 8 * (k - T), 8)
                            if k % T == T - 1:
                                attend_v(b, k // T)
                        if more:
                            for n in range(T):
                                v_unit(b + 1, n)

                    qk_matmuls(0, 0, 96, begin=True)
                    for n in range(T):
                        v_unit(0, n)
                    scores(0, 0)
                    scores(0, 1)
                    batch(0, last_part=False)
                    with pe.Fori(1, B - 1, 1) as b:
                        batch(b)
                    batch(B - 1, more=False)
                    for n in range(T):
                        project(B, n)

                @block.scalar
                def _(act):
                    def exponent(b, k):
                        for a in range(2):
                            act.wait_ge(max_found, b * 32 + (2 * k + a + 1))
                            act.activation(probs[:, k % 2, a, :], probs[:, k % 2, a, :], ACT.Exp,
                                           bias=bias_row[:, k % 4, a:a + 1], scale=-1.0,
                                           accum_out=sums[:, k % 4, a:a + 1]).then_inc(exp_made, 1)

                    def pt_hi_part(b, k):
                        n = k % T
                        for a in range(2):
                            act.wait_ge(probs_turned, b * 32 + (2 * k + a + 1))
                            act.activation(pt_hi[:, a, :, n * P:(n + 1) * P],
                                           t_bank[a][:].rearrange("p (m n) -> p m n", m=T), ACT.Copy)\
                                .then_inc(pthi_made, 1)

                    def qk_hi_part(b, i):
                        act.wait_ge(qkv_done, b * 12 + (i + 1))
                        act.activation((q_hi, k_hi)[i % 2][:, i // 2, :], g_bank[i % 2][:], ACT.Copy)\
                            .then_inc(qkvhi_made, 1)

                    def v_hi_part(b, n):
                        act.wait_ge(qkv_done, b * 12 + (n + 9))
                        act.activation(v[:, n, :, 0, :], g_bank[n % 2][:].rearrange("p (h d) -> p h d", d=HEAD),
                                       ACT.Copy).then_inc(qkvhi_made, 1)

                    def ot_halves(b, p):
                        act.wait_ge(pv_done, b * 8 + (2 * p + 1))
                        if not (isinstance(b, int) and b * PAIRS + p == 0):
                            act.wait_ge(otlo_made, b * 4 + p)
                        act.activation(ot[0:HEAD, :], o_bank[0][HEAD:P, :], ACT.Copy).then_inc(ot_half, 1)
                        act.wait_ge(pv_done, b * 8 + (2 * p + 2))
                        act.activation(ot[HEAD:P, :], o_bank[1][0:HEAD, :], ACT.Copy).then_inc(ot_half, 1)

                    def ot_hi_part(b, p):
                        act.wait_ge(ot_summed, b * 8 + (2 * p + 2))
                        act.activation(ot_hi[:, p, :], ot[:], ACT.Copy).then_inc(othi_made, 1)

                    def result(b, n):
                        act.wait_ge(shift_made, b * 4 + (n - 3))
                        act.activation(o[:, n, :], t[:], ACT.Identity, bias=shift[:, n:n + 1],
                                       scale=rstd[:, n, 1:2]).then_inc(y_made, 1)

                    def batch(b, attend=True, last_part=True, more=True):
                        for k in range(STEPS):
                            if attend:
                                pt_hi_part(b, k)
                            if last_part and row_at(k - 3) is not None:
                                result(b, row_at(k - 3))
                            if attend and (k + 2 < STEPS or more):
                                exponent(b, k + 2)
                            if attend and k % T == 0 and k > 0:
                                ot_halves(b, k // T - 1)
                            if attend and k % T == 2 and k > T:
                                ot_hi_part(b, k // T - 1)
                            if attend and more and k in unit_step:
                                qk_hi_part(b + 1, unit_step.index(k))
                        if attend:
                            ot_halves(b, PAIRS - 1)
                            ot_hi_part(b, PAIRS - 1)
                        if last_part:
                            result(b, T - 1)
                        if attend and more:
                            for n in range(T):
                                v_hi_part(b + 1, n)

                    for i in range(QK):
                        qk_hi_part(0, i)
                    for n in range(T):
                        v_hi_part(0, n)
                    exponent(0, 0)
                    exponent(0, 1)
                    batch(0, last_part=False)
                    with act.Fori(1, B - 1, 1) as b:
                        batch(b)
                    batch(B - 1, more=False)
                    batch(B, attend=False)

                @block.vector
                def _(dve):
                    def masked_max(b, k, waited=False):
                        if not waited:
                            dve.wait_ge(scores_made, b * 32 + (2 * k + 2))
                        for a in range(2):
                            dve.tensor_tensor_reduce(probs[:, k % 2, a, :], s_bank[a][:], mask_bias[:, k % T, :],
                                                     -SCALE, 3.0e38, ALU.add, ALU.min,
                                                     bias_row[:, k % 4, a:a + 1]).then_inc(max_found, 1)

                    def inverse(b, k):
                        dve.wait_ge(exp_made, b * 32 + (2 * k + 2))
                        dve.reciprocal(inv_sums[:, k % 4, :], sums[:, k % 4, :]).then_inc(inv_made, 1)

                    def pt_lo_part(b, k, scores_too):
                        cols = slice(k % T * P, (k % T + 1) * P)
                        for a in range(2):
                            dve.wait_ge(pthi_made, b * 32 + (2 * k + a + 1))
                            if a == 1 and scores_too:
                                dve.wait_ge(scores_made, b * 32 + (2 * k + 6))
                            dve.tensor_tensor(pt_lo[:, a, :, cols], t_bank[a][:].rearrange("p (m n) -> p m n", m=T),
                                              f32(pt_hi[:, a, :, cols]), ALU.subtract).then_inc(ptlo_made, 1)

                    def qk_lo_part(b, i):
                        dve.wait_ge(qkvhi_made, b * 12 + (i + 1))
                        hi, lo = ((q_hi, q_lo), (k_hi, k_lo))[i % 2]
                        dve.tensor_tensor(lo[:, i // 2, :], g_bank[i % 2][:], f32(hi[:, i // 2, :]), ALU.subtract)\
                            .then_inc(qkvlo_made, 1)

                    def v_lo_part(b, n):
                        dve.wait_ge(qkvhi_made, b * 12 + (n + 9))
                        dve.tensor_tensor(v[:, n, :, 1, :], g_bank[n % 2][:].rearrange("p (h d) -> p h d", d=HEAD),
                                          f32(v[:, n, :, 0, :]), ALU.subtract).then_inc(qkvlo_made, 1)

                    def ot_sum(b, p):
                        for a in range(2):
                            dve.wait_ge(ot_half, b * 8 + (2 * p + a + 1))
                            h = slice(a * HEAD, (a + 1) * HEAD)
                            dve.tensor_tensor(ot[h, :], o_bank[a][h, :], ot[h, :], ALU.add).then_inc(ot_summed, 1)

                    def ot_lo_part(b, p):
                        dve.wait_ge(othi_made, b * 4 + (p + 1))
                        dve.tensor_tensor(ot_lo[:, p, :], ot[:], f32(ot_hi[:, p, :]), ALU.subtract)\
                            .then_inc(otlo_made, 1)

                    def statistics(b, n, i, rows_of):
                        dve.bn_stats(stats[:, n, i, :], rows_of).then_inc(stats_made[i], 1)
                        dve.wait_ge(stats_made[i], 1)
                        dve.wait_ge(stats_made[i], b * 4 + (n - 3))
                        dve.bn_aggr(mean_var[:, n, i, :], stats[:, n, i, :]).then_inc(mean_made[i], 1)
                        dve.wait_ge(mean_made[i], b * 4 + (n - 3))
                        dve.tensor_scalar(var_eps[:, n, i:i + 1], mean_var[:, n, i, 1:2], EPS, None, ALU.add)\
                            .then_inc(eps_added[i], 1)

                    def row_shift(b, n):
                        dve.wait_ge(rstd_made[1], b * 4 + (n - 3))
                        dve.tensor_scalar(shift[:, n:n + 1], mean_var[:, n, 1, 0:1], rstd[:, n, 1:2], -1.0,
                                          ALU.mult, ALU.mult).then_inc(shift_made, 1)

                    def add_bproj(b, n):
                        dve.wait_ge(proj_done, b * 4 + (n - 3))
                        if not (isinstance(b, int) and b == 1):
                            dve.wait_ge(y_stored, b * 64 + 16 * (n - 7))
                        dve.tensor_tensor(o[:, n, :], g_bank[n % 2][:], bproj_row[:], ALU.add).then_inc(o_made, 1)
                        dve.wait_ge(o_made, b * 4 + (n - 3))
                        statistics(b, n, 0, o[:, n, :])

                    def add_layernorm(b, n):
                        if not (isinstance(b, int) and b == 1 and n == 0):
                            dve.wait_ge(y_made, b * 4 + (n - 4))
                        dve.scalar_tensor_tensor(out=t[:], in0=o[:, n, :], scalar=mean_var[:, n, 0, 0:1],
                                                 in1=gamma_row[:], op0=ALU.subtract, op1=ALU.mult)\
                            .then_inc(gamma_done, 1)
                        dve.wait_ge(rstd_made[0], b * 4 + (n - 3))
                        dve.wait_ge(gamma_done, b * 4 + (n - 3))
                        dve.scalar_tensor_tensor(out=t[:], in0=t[:], scalar=rstd[:, n, 0:1], in1=o[:, n, :],
                                                 op0=ALU.mult, op1=ALU.add).then_inc(o_added, 1)

                    def sums_in(k):
                        return k % T == 1 and k > T

                    def last_statistics(b, n):
                        dve.wait_ge(u_added, b * 4 + (n - 3))
                        statistics(b, n, 1, t[:])

                    def batch(b, attend=True, last_part=True, more=True):
                        for k in range(STEPS):
                            ahead = attend and (k + 2 < STEPS or more)
                            if attend and (k + 1 < STEPS or more) and not sums_in(k - 1):
                                inverse(b, k + 1)
                            if attend and more and k - 1 in unit_step:
                                qk_lo_part(b + 1, unit_step.index(k - 1))
                            if attend:
                                pt_lo_part(b, k, ahead)
                            if last_part and row_at(k - 3) is not None:
                                row_shift(b, row_at(k - 3))
                            if ahead:
                                masked_max(b, k + 2, waited=True)
                            if last_part and k < T:
                                add_bproj(b, k)
                            if last_part and row_at(k) is not None:
                                add_layernorm(b, row_at(k))
                            if last_part and row_at(k - 2) is not None:
                                last_statistics(b, row_at(k - 2))
                            if attend and sums_in(k):
                                if ahead:
                                    inverse(b, k + 2)
                                ot_sum(b, k // T - 1)
                            if attend and k % T == 3 and k > T:
                                ot_lo_part(b, k // T - 1)
                        if attend and more:
                            qk_lo_part(b + 1, QK - 1)
                        if attend:
                            ot_sum(b, PAIRS - 1)
                        if last_part:
                            last_statistics(b, T - 1)
                        if attend:
                            ot_lo_part(b, PAIRS - 1)
                        if last_part:
                            row_shift(b, T - 1)
                        if attend and more:
                            for n in range(T):
                                v_lo_part(b + 1, n)

                    for i in range(QK):
                        qk_lo_part(0, i)
                    for n in range(T):
                        v_lo_part(0, n)
                    masked_max(0, 0)
                    masked_max(0, 1)
                    inverse(0, 0)
                    batch(0, last_part=False)
                    batch(1)
                    with dve.Fori(2, B - 1, 1) as b:
                        batch(b)
                    batch(B - 1, more=False)
                    batch(B, attend=False)


_INS = ["x", "adj", "L0_gnn_weight", "L0_gnn_bias", "L1_gnn_w_qkv", "L1_gnn_w_proj", "L1_gnn_b_proj",
        "L1_gnn_ln_gamma", "L1_gnn_ln_beta"]


def kernel(**inputs):
    import numpy as _np
    import concourse.bacc as _bacc
    from concourse import mybir as _mybir
    from concourse.bass_utils import run_bass_kernel_spmd as _run

    nc = _bacc.Bacc("TRN2", target_bir_lowering=False, num_devices=1)
    arrays, args = {}, []
    for name in _INS:
        a = _np.ascontiguousarray(inputs[name])
        arrays[f"in_{name}_dram"] = a
        args.append(nc.dram_tensor(f"in_{name}_dram", a.shape, _mybir.dt.from_np(a.dtype), kind="ExternalInput").ap())
    shape = arrays["in_x_dram"].shape
    out = nc.dram_tensor("out_0_dram", shape, _mybir.dt.float32, kind="ExternalOutput").ap()
    graph_layers(nc, *args, out)
    r = _run(nc, [arrays], core_ids=[0])
    return r.results[0]["out_0_dram"]
```

```python
from contextlib import ExitStack

import concourse.bass as bass
from concourse import mybir

F32 = mybir.dt.float32
F32R = mybir.dt.float32r
BF16 = mybir.dt.bfloat16
ALU = mybir.AluOpType
ACT = mybir.ActivationFunctionType
P = 128
EPS = 1e-5
MASKED = -1.0e30


def graph_layers(nc, x, adj, w0, b0, wqkv, wproj, bproj, gamma, beta, out):
    B, N, D = x.shape
    T = N // P
    HEAD = 64
    PAIRS = D // (2 * HEAD)
    SCALE = float(HEAD) ** -0.5
    assert N == 512 and D == 512 and T == 4 and PAIRS == 4

    ub_dram = nc.dram_tensor("u_beta_rows", [B, N, D], F32, kind="Internal").ap()
    uth_dram = nc.dram_tensor("ut_hi", [B, T, P, T, P], F32, kind="Internal").ap()
    utl_dram = nc.dram_tensor("ut_lo", [B, T, P, T, P], F32, kind="Internal").ap()

    def rows(m):
        return m.rearrange("(t p) d -> p t d", p=P)

    def f32(ap):
        return ap.bitcast(F32)

    with ExitStack() as whole:
        def keep(name, shape, dt):
            return whole.enter_context(nc.sbuf_tensor(name, shape, dt))

        w_hi = keep("w_hi", [P, 4, T, D], F32R)
        w_lo = keep("w_lo", [P, 4, T, D], F32R)
        mask_bias = keep("mask_bias", [P, T, N], BF16)
        ident = keep("ident", [P, P], F32)
        half_neg = keep("half_neg", [P, 1], F32)
        bproj_row = keep("bproj_row", [P, D], F32)
        gamma_row = keep("gamma_row", [P, D], F32)

        x_hi = keep("x_hi", [P, T, D], F32R)
        x_lo = keep("x_lo", [P, T, D], F32R)
        xt_hi, xt_lo = x_hi, x_lo
        xt_loaded = whole.enter_context(nc.semaphore("xt_loaded"))

        psum = [whole.enter_context(nc.psum_tensor(f"bank{i}", [P, 512], F32)) for i in range(8)]

        def load_u_turned(sp, b):
            for j in range(T):
                cols = slice(j * P, (j + 1) * P)
                sp.dma_start(f32(xt_hi[:, :, cols]), uth_dram[b, j]).then_inc(xt_loaded, 16)
                sp.dma_start(f32(xt_lo[:, :, cols]), utl_dram[b, j]).then_inc(xt_loaded, 16)

        with ExitStack() as first:
            def sb(name, shape, dt):
                return first.enter_context(nc.sbuf_tensor(name, shape, dt))

            def sem(name):
                return first.enter_context(nc.semaphore(name))

            adjt_hi = sb("adjt_hi", [P, T, N], F32R)
            adjt_lo = sb("adjt_lo", [P, T, N], F32R)
            w0_hi = sb("w0_hi", [P, T, D], F32R)
            w0_lo = sb("w0_lo", [P, T, D], F32R)
            b0_row = sb("b0_row", [P, D], F32)
            beta_row = sb("beta_row", [P, D], F32)
            x_in = sb("x_in", [P, T, D], F32)
            xb = sb("xb", [P, T, D], F32)
            yt_hi = sb("yt_hi", [P, T, N], F32R)
            yt_lo = sb("yt_lo", [P, T, N], F32R)
            res = sb("res", [P, 2, D], F32)
            u = sb("u", [P, T, D], F32)
            ub = sb("ub", [P, T, D], F32)
            ut_hi = sb("ut_hi_sb", [P, T, N], F32R)
            ut_lo = sb("ut_lo_sb", [P, T, N], F32R)
            stats = sb("stats", [P, T, 6], F32)
            mean_var = sb("mean_var", [P, T, 2], F32)
            var_eps = sb("var_eps", [P, T], F32)
            rstd = sb("rstd", [P, T], F32)
            shift = sb("shift", [P, T], F32)

            w_in = sb("w_in", [P, T, D], F32)
            adj_in, w0_in = u, ub

            ident_made = sem("ident_made")
            adj_loaded = sem("adj_loaded")
            x_loaded = sem("x_loaded")
            w0_loaded = sem("w0_loaded")
            b0_loaded = sem("b0_loaded")
            rows_loaded = sem("rows_loaded")
            w_loaded = [sem(f"w_loaded{i}") for i in range(T)]
            adj_turned = sem("adj_turned")
            adjt_hi_made = sem("adjt_hi_made")
            adjt_lo_made = sem("adjt_lo_made")

            w_dram = [rows(wqkv[:, i * D:(i + 1) * D]) for i in range(3)] + [rows(wproj)]
            W_TILES = 4 * T

            def load_w(sp, g):
                sp.dma_start(w_in[:, g % T, :], w_dram[g // T][:, g % T, :]).then_inc(w_loaded[g % T], 16)

            with nc.Block() as block:
                @block.sync
                def _(sp):
                    sp.dma_start(adj_in[:], rows(adj)).then_inc(adj_loaded, 16)
                    sp.dma_start(x_in[:], rows(x[0])).then_inc(x_loaded, 16)
                    sp.dma_start(w0_in[:], rows(w0)).then_inc(w0_loaded, 16)
                    sp.dma_start(b0_row[:], b0.partition_broadcast(P)).then_inc(b0_loaded, 16)
                    for g in range(T):
                        load_w(sp, g)
                    for row, src in ((beta_row, beta), (bproj_row, bproj), (gamma_row, gamma)):
                        sp.dma_start(row[:], src.partition_broadcast(P)).then_inc(rows_loaded, 16)

                @block.gpsimd
                def _(pool):
                    pool.memset(half_neg[:], -0.5)
                    pool.memset(ident[:], 0.0).then_inc(ident_made, 1)
                    pool.wait_ge(ident_made, 1)
                    pool.affine_select(out=ident[:], in_=ident[:], compare_op=ALU.not_equal, fill=1.0, base=0,
                                       pattern=[[-1, P]], channel_multiplier=1).then_inc(ident_made, 1)

                @block.tensor
                def _(pe):
                    pe.wait_ge(ident_made, 2)
                    pe.wait_ge(adj_loaded, 16)
                    for m in range(T):
                        for n in range(T):
                            last = pe.transpose(psum[m][:, n * P:(n + 1) * P], adj_in[:, n, m * P:(m + 1) * P],
                                                ident[:])
                        last.then_inc(adj_turned, 1)

                @block.scalar
                def _(act):
                    for m in range(T):
                        act.wait_ge(adj_turned, m + 1)
                        act.activation(adjt_hi[:, m, :], psum[m][:], ACT.Copy).then_inc(adjt_hi_made, 1)

                @block.vector
                def _(dve):
                    dve.wait_ge(adj_loaded, 16)
                    dve.tensor_scalar(mask_bias[:], adj_in[:], 0.0, MASKED, ALU.is_equal, ALU.mult)
                    for m in range(T):
                        dve.wait_ge(adjt_hi_made, m + 1)
                        dve.tensor_tensor(adjt_lo[:, m, :], psum[m][:], f32(adjt_hi[:, m, :]), ALU.subtract)\
                            .then_inc(adjt_lo_made, 1)

            w0hi_made = sem("w0hi_made")
            w0lo_made = sem("w0lo_made")
            whi_made = sem("whi_made")
            wlo_made = sem("wlo_made")
            xhi_made = sem("xhi_made")
            xlo_made = sem("xlo_made")
            xb_made = sem("xb_made")
            yz_done = sem("yz_done")
            yhi_made = sem("yhi_made")
            ylo_made = sem("ylo_made")
            res_made = sem("res_made")
            stats_made = sem("stats_made")
            mean_made = sem("mean_made")
            eps_added = sem("eps_added")
            rstd_made = sem("rstd_made")
            shift_made = sem("shift_made")
            u_made = sem("u_made")
            u_turned = sem("u_turned")
            uthi_made = sem("uthi_made")
            utlo_made = sem("utlo_made")
            ub_made = sem("ub_made")
            ub_stored = sem("ub_stored")
            ut_stored = [sem(f"ut_stored{j}") for j in range(T)]

            yz_bank = psum[0:4]
            turn_bank = psum[4:6]

            with nc.Block() as block:
                @block.sync
                def _(sp):
                    def store_ut(b, j):
                        cols = slice(j * P, (j + 1) * P)
                        sp.wait_ge(utlo_made, b * 4 + (j + 1))
                        sp.dma_start(uth_dram[b, j], f32(ut_hi[:, :, cols])).then_inc(ut_stored[j], 16)
                        sp.dma_start(utl_dram[b, j], f32(ut_lo[:, :, cols])).then_inc(ut_stored[j], 16)

                    def store_ub(b):
                        sp.wait_ge(ub_made, b * 4 + 4)
                        sp.dma_start(rows(ub_dram[b]), ub[:]).then_inc(ub_stored, 16)

                    def load_x(b):
                        sp.wait_ge(xb_made, b * 4)
                        sp.dma_start(x_in[:], rows(x[b])).then_inc(x_loaded, 16)

                    def more_w(first):
                        for g in range(first, first + T):
                            sp.wait_ge(wlo_made, g - 3)
                            load_w(sp, g)

                    def batch(b, first=False, last=False):
                        if not last:
                            load_x(b + 1)
                        if not first:
                            store_ub(b - 1)
                            store_ut(b - 1, 2)
                            store_ut(b - 1, 3)
                        if isinstance(b, int) and b < 2:
                            more_w(4 + 8 * b)
                        if last:
                            sp.wait_ge(yz_done, b * 8 + 4)
                            for j in range(T):
                                sp.wait_ge(ut_stored[j], 32)
                            load_u_turned(sp, 0)
                        store_ut(b, 0)
                        store_ut(b, 1)
                        if isinstance(b, int) and b == 0:
                            more_w(8)

                    batch(0, first=True)
                    batch(1)
                    with sp.Fori(2, B - 1, 1) as b:
                        batch(b)
                    batch(B - 1, last=True)
                    store_ub(B - 1)
                    store_ut(B - 1, 2)
                    store_ut(B - 1, 3)
                    sp.wait_ge(ub_stored, 16 * B)
                    for j in range(T):
                        sp.wait_ge(ut_stored[j], 32 * B)

                @block.gpsimd
                def _(pool):
                    def add_beta(b, j, first):
                        pool.wait_ge(u_made, b * 4 + (j + 1))
                        if j == 0 and not first:
                            pool.wait_ge(ub_stored, b * 16)
                        pool.tensor_tensor(ub[:, j, :], u[:, j, :], beta_row[:], ALU.add).then_inc(ub_made, 1)

                    def add_b0(b, j):
                        pool.wait_ge(xlo_made, b * 4 + (j + 1))
                        if not (isinstance(b, int) and b == 0):
                            pool.wait_ge(res_made, b * 4 + (j - 3))
                        pool.tensor_tensor(xb[:, j, :], x_in[:, j, :], b0_row[:], ALU.add).then_inc(xb_made, 1)

                    def batch(b, first=False, last=False):
                        for j in range(T):
                            pool.wait_ge(eps_added, b * 4 + (j + 1))
                            pool.tensor_tensor(rstd[:, j:j + 1], var_eps[:, j:j + 1], half_neg[:], ALU.pow)\
                                .then_inc(rstd_made, 1)
                            if not last:
                                add_b0(b + 1, j)
                        for j in range(T):
                            add_beta(b, j, first)

                    pool.wait_ge(b0_loaded, 16)
                    for j in range(T):
                        add_b0(0, j)
                    pool.wait_ge(rows_loaded, 48)
                    batch(0, first=True)
                    with pool.Fori(1, B - 1, 1) as b:
                        batch(b)
                    batch(B - 1, last=True)

                @block.tensor
                def _(pe):
                    def y(b, j, first=False):
                        bank = yz_bank[j]
                        if not first:
                            pe.wait_ge(res_made, b * 4 + (j - 3))
                        n = 0
                        for a, c in ((x_hi, adjt_hi), (x_hi, adjt_lo), (x_lo, adjt_hi)):
                            if j == 0 and c is adjt_hi:
                                pe.wait_ge(xhi_made if a is x_hi else xlo_made, b * 4 + 4)
                            for m in range(T):
                                last = pe.matmul(bank[:], a[:, m, j * P:(j + 1) * P], c[:, m, :],
                                                 start=n == 0, stop=n == 11)
                                n += 1
                        last.then_inc(yz_done, 1)

                    def z(b, j):
                        bank = yz_bank[j]
                        if isinstance(b, int) and b == 0 and j == 0:
                            pe.wait_ge(w0lo_made, T)
                        for m in range(T):
                            if j == 0:
                                pe.wait_ge(ylo_made, b * 4 + (m + 1))
                            for i, (a, c) in enumerate(((yt_hi, w0_hi), (yt_hi, w0_lo), (yt_lo, w0_hi))):
                                last = pe.matmul(bank[:], a[:, m, j * P:(j + 1) * P], c[:, m, :],
                                                 start=m == 0 and i == 0, stop=m == 3 and i == 2)
                        last.then_inc(yz_done, 1)

                    def turn(b, j, free=True):
                        pe.wait_ge(u_made, b * 4 + (j + 1))
                        if free:
                            pe.wait_ge(utlo_made, b * 4 + (j - 1))
                        for d in range(T):
                            last = pe.transpose(turn_bank[j % 2][:, d * P:(d + 1) * P], u[:, j, d * P:(d + 1) * P],
                                                ident[:])
                        last.then_inc(u_turned, 1)

                    def batch(b, first=False):
                        y(b, 0, first)
                        if not first:
                            turn(b - 1, 2)
                        y(b, 1, first)
                        if not first:
                            turn(b - 1, 3)
                        y(b, 2, first)
                        y(b, 3, first)
                        z(b, 0)
                        z(b, 1)
                        z(b, 2)
                        turn(b, 0, free=not first)
                        z(b, 3)
                        turn(b, 1, free=not first)

                    batch(0, first=True)
                    with pe.Fori(1, B, 1) as b:
                        batch(b)
                    turn(B - 1, 2)
                    turn(B - 1, 3)

                @block.scalar
                def _(act):
                    def x_hi_part(b):
                        act.wait_ge(x_loaded, b * 16 + 16)
                        for m in range(T):
                            act.activation(x_hi[:, m, :], x_in[:, m, :], ACT.Copy).then_inc(xhi_made, 1)

                    def y_hi_part(b, j):
                        act.wait_ge(yz_done, b * 8 + (j + 1))
                        act.activation(yt_hi[:, j, :], yz_bank[j][:], ACT.Copy).then_inc(yhi_made, 1)

                    def normalise(b, j):
                        act.wait_ge(shift_made, b * 4 + (j + 1))
                        act.activation(u[:, j, :], res[:, j % 2, :], ACT.Identity, bias=shift[:, j:j + 1],
                                       scale=rstd[:, j:j + 1]).then_inc(u_made, 1)

                    def ut_hi_part(b, j):
                        act.wait_ge(u_turned, b * 4 + (j + 1))
                        if not (isinstance(b, int) and b == 0):
                            act.wait_ge(ut_stored[j], b * 32)
                        act.activation(ut_hi[:, :, j * P:(j + 1) * P],
                                       turn_bank[j % 2][:].rearrange("p (d n) -> p d n", d=T), ACT.Copy)\
                            .then_inc(uthi_made, 1)

                    def w0_hi_part():
                        act.wait_ge(w0_loaded, 16)
                        for m in range(T):
                            act.activation(w0_hi[:, m, :], w0_in[:, m, :], ACT.Copy).then_inc(w0hi_made, 1)

                    def w_hi_part(b, g):
                        if isinstance(b, int) and b < 2:
                            g += 8 * b
                            act.wait_ge(w_loaded[g % T], 16 * (g // T + 1))
                            act.activation(w_hi[:, g // T, g % T, :], w_in[:, g % T, :], ACT.Copy)\
                                .then_inc(whi_made, 1)

                    def batch(b, first=False, last=False):
                        for j in range(T):
                            y_hi_part(b, j)
                            w_hi_part(b, j)
                            if not first and j < 2:
                                ut_hi_part(b - 1, j + 2)
                        if not last:
                            x_hi_part(b + 1)
                        if not first:
                            act.wait_ge(ub_made, b * 4)
                            act.wait_ge(u_turned, b * 4)
                        normalise(b, 0)
                        w_hi_part(b, 4)
                        normalise(b, 1)
                        ut_hi_part(b, 0)
                        w_hi_part(b, 5)
                        normalise(b, 2)
                        ut_hi_part(b, 1)
                        w_hi_part(b, 6)
                        normalise(b, 3)
                        w_hi_part(b, 7)

                    x_hi_part(0)
                    w0_hi_part()
                    batch(0, first=True)
                    batch(1)
                    with act.Fori(2, B - 1, 1) as b:
                        batch(b)
                    batch(B - 1, last=True)
                    ut_hi_part(B - 1, 2)
                    ut_hi_part(B - 1, 3)

                @block.vector
                def _(dve):
                    def x_lo_part(b, m):
                        dve.wait_ge(xhi_made, b * 4 + (m + 1))
                        dve.tensor_tensor(x_lo[:, m, :], x_in[:, m, :], f32(x_hi[:, m, :]), ALU.subtract)\
                            .then_inc(xlo_made, 1)

                    def y_lo_part(b, j):
                        dve.wait_ge(yhi_made, b * 4 + (j + 1))
                        dve.tensor_tensor(yt_lo[:, j, :], yz_bank[j][:], f32(yt_hi[:, j, :]), ALU.subtract)\
                            .then_inc(ylo_made, 1)

                    def row_stats(b, j, free=True):
                        dve.wait_ge(yz_done, b * 8 + (j + 5))
                        dve.wait_ge(xb_made, b * 4 + (j + 1))
                        if free:
                            dve.wait_ge(u_made, b * 4 + (j - 1))
                        dve.tensor_tensor(res[:, j % 2, :], yz_bank[j][:], xb[:, j, :], ALU.add)\
                            .then_inc(res_made, 1)
                        dve.wait_ge(res_made, b * 4 + (j + 1))
                        dve.bn_stats(stats[:, j, :], res[:, j % 2, :]).then_inc(stats_made, 1)
                        dve.wait_ge(stats_made, 1)
                        dve.wait_ge(stats_made, b * 4 + (j + 1))
                        dve.bn_aggr(mean_var[:, j, :], stats[:, j, :]).then_inc(mean_made, 1)
                        dve.wait_ge(mean_made, b * 4 + (j + 1))
                        dve.tensor_scalar(var_eps[:, j:j + 1], mean_var[:, j, 1:2], EPS, None, ALU.add)\
                            .then_inc(eps_added, 1)

                    def row_shift(b, j):
                        dve.wait_ge(rstd_made, b * 4 + (j + 1))
                        dve.tensor_scalar(shift[:, j:j + 1], mean_var[:, j, 0:1], rstd[:, j:j + 1], -1.0,
                                          ALU.mult, ALU.mult).then_inc(shift_made, 1)

                    def ut_lo_part(b, j):
                        dve.wait_ge(uthi_made, b * 4 + (j + 1))
                        cols = slice(j * P, (j + 1) * P)
                        dve.tensor_tensor(ut_lo[:, :, cols], turn_bank[j % 2][:].rearrange("p (d n) -> p d n", d=T),
                                          f32(ut_hi[:, :, cols]), ALU.subtract).then_inc(utlo_made, 1)

                    def w0_lo_part():
                        for m in range(T):
                            dve.wait_ge(w0hi_made, m + 1)
                            dve.tensor_tensor(w0_lo[:, m, :], w0_in[:, m, :], f32(w0_hi[:, m, :]), ALU.subtract)\
                                .then_inc(w0lo_made, 1)

                    def w_lo_part(b, g):
                        if isinstance(b, int) and b < 2:
                            g += 8 * b
                            dve.wait_ge(whi_made, g + 1)
                            dve.tensor_tensor(w_lo[:, g // T, g % T, :], w_in[:, g % T, :],
                                              f32(w_hi[:, g // T, g % T, :]), ALU.subtract).then_inc(wlo_made, 1)

                    def batch(b, first=False, last=False):
                        for j in range(T):
                            y_lo_part(b, j)
                            w_lo_part(b, j)
                            if not first and j < 2:
                                ut_lo_part(b - 1, j + 2)
                        if not last:
                            x_lo_part(b + 1, 0)
                            x_lo_part(b + 1, 1)
                        row_stats(b, 0, free=not first)
                        if not last:
                            x_lo_part(b + 1, 2)
                        row_shift(b, 0)
                        row_stats(b, 1, free=not first)
                        if not last:
                            x_lo_part(b + 1, 3)
                        row_shift(b, 1)
                        w_lo_part(b, 4)
                        row_stats(b, 2)
                        ut_lo_part(b, 0)
                        row_shift(b, 2)
                        w_lo_part(b, 5)
                        row_stats(b, 3)
                        ut_lo_part(b, 1)
                        row_shift(b, 3)
                        w_lo_part(b, 6)
                        w_lo_part(b, 7)

                    for m in range(T):
                        x_lo_part(0, m)
                    w0_lo_part()
                    batch(0, first=True)
                    batch(1)
                    with dve.Fori(2, B - 1, 1) as b:
                        batch(b)
                    batch(B - 1, last=True)
                    ut_lo_part(B - 1, 2)
                    ut_lo_part(B - 1, 3)

        with ExitStack() as second:
            def sb(name, shape, dt):
                return second.enter_context(nc.sbuf_tensor(name, shape, dt))

            def sem(name):
                return second.enter_context(nc.semaphore(name))

            q_hi = sb("q_hi", [P, PAIRS, N], F32R)
            q_lo = sb("q_lo", [P, PAIRS, N], F32R)
            k_hi = sb("k_hi", [P, PAIRS, N], F32R)
            k_lo = sb("k_lo", [P, PAIRS, N], F32R)
            v = sb("v", [P, T, 2 * PAIRS, 2, HEAD], F32R)
            probs = sb("probs", [P, 2, 2, N], F32)
            pt_hi = sb("pt_hi", [P, 2, T, N], F32R)
            pt_lo = sb("pt_lo", [P, 2, T, N], F32R)
            ot_hi = sb("ot_hi", [P, PAIRS, N], F32R)
            ot_lo = sb("ot_lo", [P, PAIRS, N], F32R)
            ot = sb("ot", [P, N], F32)
            o = sb("o", [P, T, D], F32)
            t = sb("t", [P, D], F32)
            ub = sb("ub_row", [P, D], F32)
            bias_row = sb("bias_row", [P, 4, 2], F32)
            sums = sb("sums", [P, 4, 2], F32)
            inv_sums = sb("inv_sums", [P, 4, 2], F32)
            stats = sb("o_stats", [P, T, 2, 6], F32)
            mean_var = sb("o_mean_var", [P, T, 2, 2], F32)
            var_eps = sb("o_var_eps", [P, T, 2], F32)
            rstd = sb("o_rstd", [P, T, 2], F32)
            shift = sb("o_shift", [P, T], F32)

            s_bank, t_bank, o_bank, g_bank = psum[0:2], psum[2:4], psum[4:6], psum[6:8]

            STEPS = PAIRS * T
            STRIP = 32
            scores_made = sem("scores_made")
            max_found = sem("max_found")
            exp_made = sem("exp_made")
            inv_made = sem("inv_made")
            probs_made = sem("probs_made")
            probs_turned = sem("probs_turned")
            pthi_made = sem("pthi_made")
            ptlo_made = sem("ptlo_made")
            pv_done = sem("pv_done")
            ot_half = sem("ot_half")
            ot_summed = sem("ot_summed")
            othi_made = sem("othi_made")
            otlo_made = sem("otlo_made")
            qk_done = sem("qk_done")
            qkhi_made = sem("qkhi_made")
            qklo_made = sem("qklo_made")
            v_done = sem("v_done")
            vhi_made = sem("vhi_made")
            vlo_made = sem("vlo_made")
            proj_done = sem("proj_done")
            o_made = sem("o_made")
            stats_made = [sem(f"o_stats_made{i}") for i in range(2)]
            mean_made = [sem(f"o_mean_made{i}") for i in range(2)]
            eps_added = [sem(f"o_eps_added{i}") for i in range(2)]
            rstd_made = [sem(f"o_rstd_made{i}") for i in range(2)]
            shift_made = sem("o_shift_made")
            gamma_done = sem("gamma_done")
            o_added = sem("o_added")
            u_loaded = sem("u_loaded")
            last_u_loaded = sem("last_u_loaded")
            u_added = sem("u_added")
            y_made = sem("y_made")
            y_stored = sem("y_stored")

            O_STEP = [4, 5, 6, 7]
            LN_STEP = [7, 9, 11, 13]
            assert LN_STEP[-1] + 2 < STEPS

            def rows_of(b, n):
                if isinstance(b, int) and b == B:
                    return probs[:, n // 2, n % 2, :], f32(xt_lo[:, n, :])
                return t[:], ub[:]

            def row_at(k, steps):
                return steps.index(k) if k in steps else None

            def output_at(b, k, j):
                if j == 2 and k == 6:
                    return None
                if k % T == j or (j == 2 and k == 7):
                    return (b - 1, PAIRS - 1) if k < T else (b, k // T - 1)
                return None

            with nc.Block() as block:
                @block.sync
                def _(sp):
                    def load_xt(b):
                        sp.wait_ge(v_done, b * 4)
                        load_u_turned(sp, b)

                    def load_ub(b, n, loaded=u_loaded):
                        sp.dma_start(rows_of(b, n)[1], ub_dram[b - 1, n * P:(n + 1) * P, :]).then_inc(loaded, 16)

                    def finish(b, last=False):
                        for n in range(T):
                            sp.wait_ge(y_made, b * 4 + (n - 3))
                            if not last and not (isinstance(b, int) and b == B - 1 and n == T - 1):
                                load_ub(b + (n + 1) // T, (n + 1) % T)
                            sp.dma_start(out[b - 1, n * P:(n + 1) * P, :], o[:, n, :]).then_inc(y_stored, 16)

                    load_ub(1, 0)
                    load_xt(1)
                    with sp.Fori(1, B - 1, 1) as b:
                        load_xt(b + 1)
                        finish(b)
                    sp.wait_ge(v_done, B * 4)
                    for n in range(T):
                        load_ub(B, n, last_u_loaded)
                    finish(B - 1)
                    finish(B, last=True)
                    sp.wait_ge(y_stored, 64 * B)

                @block.gpsimd
                def _(pool):
                    def normalise(b, k):
                        pool.wait_ge(inv_made, b * STEPS + (k + 1))
                        strip, rest = slice(0, STRIP), slice(STRIP, N)
                        pool.tensor_tensor(probs[:, k % 2, 0, strip], probs[:, k % 2, 0, strip],
                                           inv_sums[:, k % 4, 0:1].to_broadcast((P, STRIP)), ALU.mult)
                        for a, cols in ((0, rest), (1, slice(0, N))):
                            pool.tensor_scalar(probs[:, k % 2, a, cols], probs[:, k % 2, a, cols],
                                               inv_sums[:, k % 4, a:a + 1], 0.0, ALU.mult, ALU.add)\
                                .then_inc(probs_made, 1)

                    def power(b, n, i):
                        pool.wait_ge(eps_added[i], b * 4 + (n - 3))
                        pool.tensor_tensor(rstd[:, n, i:i + 1], var_eps[:, n, i:i + 1], half_neg[:], ALU.pow)\
                            .then_inc(rstd_made[i], 1)

                    def add_ub(b, n):
                        if isinstance(b, int) and b == B:
                            pool.wait_ge(last_u_loaded, 64)
                        else:
                            pool.wait_ge(u_loaded, b * 64 + 16 * (n - 3))
                        pool.wait_ge(o_added, b * 4 + (n - 3))
                        t_row, ub_row = rows_of(b, n)
                        pool.tensor_tensor(t_row, t_row, ub_row, ALU.add).then_inc(u_added, 1)

                    def batch(b, last_part=True, more=True):
                        for k in range(STEPS):
                            if last_part and row_at(k - 2, LN_STEP) is not None:
                                power(b, row_at(k - 2, LN_STEP), 1)
                            if k + 1 < STEPS or more:
                                normalise(b, k + 1)
                            if last_part and row_at(k - 1, LN_STEP) is not None:
                                add_ub(b, row_at(k - 1, LN_STEP))
                            if last_part and row_at(k, O_STEP) is not None:
                                power(b, row_at(k, O_STEP), 0)

                    normalise(0, 0)
                    batch(0, last_part=False)
                    with pool.Fori(1, B - 1, 1) as b:
                        batch(b)
                    batch(B - 1, more=False)
                    for i in range(T + 3):
                        if i < T:
                            power(B, i, 0)
                        if 0 <= i - 1 < T:
                            add_ub(B, i - 1)
                        if 0 <= i - 2 < T:
                            power(B, i - 2, 1)

                @block.tensor
                def _(pe):
                    def scores(b, k):
                        pair, n = k // T % PAIRS, k % T
                        if n == 0:
                            pe.wait_ge(qklo_made, (b + k // STEPS) * 8 + (2 * pair + 2))
                        parts = ((q_hi, k_hi), (q_hi, k_lo), (q_lo, k_hi))
                        for a in range(2):
                            if not (isinstance(b, int) and b * STEPS + k == 0):
                                pe.wait_ge(max_found, b * 32 + (2 * k + a - 1))
                        for i, (l, r) in enumerate(parts):
                            for a in range(2):
                                h = slice(a * HEAD, (a + 1) * HEAD)
                                last = pe.matmul(s_bank[a][:], l[h, pair, n * P:(n + 1) * P], r[h, pair, :],
                                                 start=i == 0, stop=i == 2)
                                if i == 2:
                                    last.then_inc(scores_made, 1)

                    def turn(b, k):
                        for a in range(2):
                            pe.wait_ge(probs_made, b * 32 + (2 * k + a + 1))
                            if not (isinstance(b, int) and b * STEPS + k == 0):
                                pe.wait_ge(ptlo_made, b * 32 + (2 * k + a - 1))
                            for m in range(T):
                                last = pe.transpose(t_bank[a][:, m * P:(m + 1) * P],
                                                    probs[:, k % 2, a, m * P:(m + 1) * P], ident[:])
                            last.then_inc(probs_turned, 1)

                    def attend_v(b, p):
                        for a in range(2):
                            pe.wait_ge(ptlo_made, b * 32 + (8 * p + 7 + a))
                            if a == 0:
                                if p == 0:
                                    pe.wait_ge(vlo_made, b * 4 + 4)
                                if not (isinstance(b, int) and b * PAIRS + p == 0):
                                    pe.wait_ge(ot_summed, b * 8 + 2 * p)
                            for m in range(T):
                                w = v[:, m, 2 * p + a, :, :].rearrange("p s d -> p (s d)")
                                pe.matmul(o_bank[a][:], w, pt_hi[:, a, m, :], start=m == 0, stop=False)
                                last = pe.matmul(o_bank[a][:], w, pt_lo[:, a, m, :], start=False, stop=m == T - 1)
                            last.then_inc(pv_done, 1)

                    def qk_matmuls(b, first, count, begin=False):
                        for g in range(first, first + count):
                            i, (m, s) = g // 12, divmod(g % 12, 3)
                            if g == 0:
                                pe.wait_ge(xt_loaded, b * 128 + 128)
                            if g % 12 == 0:
                                if i >= 2:
                                    pe.wait_ge(qklo_made, b * 8 + (i - 1))
                                elif not begin and isinstance(b, int) and b == 1:
                                    pe.wait_ge(vlo_made, 3 + i)
                                elif not begin:
                                    pe.wait_ge(o_made, b * 4 + (i - 5))
                            pair, w = i // 2, i % 2
                            a, c = ((w_hi, xt_hi), (w_hi, xt_lo), (w_lo, xt_hi))[s]
                            last = pe.matmul(g_bank[i % 2][:], a[:, w, m, pair * P:(pair + 1) * P], c[:, m, :],
                                             start=g % 12 == 0, stop=g % 12 == 11)
                            if g % 12 == 11:
                                last.then_inc(qk_done, 1)

                    def v_matmuls(b, first, count):
                        for g in range(first, first + count):
                            n, (m, s) = g // 12, divmod(g % 12, 3)
                            if g % 12 == 0:
                                if n < 2:
                                    pe.wait_ge(qklo_made, b * 8 + (7 + n))
                                else:
                                    pe.wait_ge(vlo_made, b * 4 + (n - 1))
                            a, c = ((xt_hi, w_hi), (xt_hi, w_lo), (xt_lo, w_hi))[s]
                            last = pe.matmul(g_bank[n % 2][:], a[:, m, n * P:(n + 1) * P], c[:, 2, m, :],
                                             start=g % 12 == 0, stop=g % 12 == 11)
                            if g % 12 == 11:
                                last.then_inc(v_done, 1)

                    def project(b, first, count):
                        for g in range(first, first + count):
                            n, (p, s) = g // 12, divmod(g % 12, 3)
                            if g % 12 == 0:
                                if n >= 2:
                                    pe.wait_ge(o_made, b * 4 + (n - 5))
                                elif isinstance(b, int) and b == B:
                                    pe.wait_ge(o_made, 4 * (B - 1) + n - 1)
                                else:
                                    pe.wait_ge(vlo_made, b * 4 + (3 + n))
                            if n == 0 and s == 0 and p >= PAIRS - 2:
                                pe.wait_ge(otlo_made, b * 4 + (p - 3))
                            a, c = ((ot_hi, w_hi), (ot_hi, w_lo), (ot_lo, w_hi))[s]
                            last = pe.matmul(g_bank[n % 2][:], a[:, p, n * P:(n + 1) * P], c[:, 3, p, :],
                                             start=g % 12 == 0, stop=g % 12 == 11)
                            if g % 12 == 11:
                                last.then_inc(proj_done, 1)

                    def batch(b, last_part=True, more=True):
                        for k in range(STEPS):
                            turn(b, k)
                            if k + 2 < STEPS or more:
                                scores(b, k + 2)
                            group, part = divmod(k, T)
                            if part == T - 1:
                                attend_v(b, group)
                            elif group == 0:
                                v_matmuls(b, 16 * part, 16)
                            elif group == 1 and last_part:
                                project(b, 16 * part, 16)
                            elif group >= 2 and more:
                                qk_matmuls(b + 1, 48 * (group - 2) + 16 * part, 16)

                    qk_matmuls(0, 0, 96, begin=True)
                    scores(0, 0)
                    scores(0, 1)
                    batch(0, last_part=False)
                    with pe.Fori(1, B - 1, 1) as b:
                        batch(b)
                    batch(B - 1, more=False)
                    project(B, 0, 48)

                @block.scalar
                def _(act):
                    def exponent(b, k):
                        for a in range(2):
                            act.wait_ge(max_found, b * 32 + (2 * k + a + 1))
                            act.activation(probs[:, k % 2, a, :], probs[:, k % 2, a, :], ACT.Exp,
                                           bias=bias_row[:, k % 4, a:a + 1], scale=-1.0,
                                           accum_out=sums[:, k % 4, a:a + 1]).then_inc(exp_made, 1)

                    def pt_hi_part(b, k):
                        n = k % T
                        for a in range(2):
                            act.wait_ge(probs_turned, b * 32 + (2 * k + a + 1))
                            act.activation(pt_hi[:, a, :, n * P:(n + 1) * P],
                                           t_bank[a][:].rearrange("p (m n) -> p m n", m=T), ACT.Copy)\
                                .then_inc(pthi_made, 1)

                    def qk_hi_part(b, i):
                        act.wait_ge(qk_done, b * 8 + (i + 1))
                        act.activation((q_hi, k_hi)[i % 2][:, i // 2, :], g_bank[i % 2][:], ACT.Copy)\
                            .then_inc(qkhi_made, 1)

                    def v_hi_part(b, n):
                        act.wait_ge(v_done, b * 4 + (n + 1))
                        act.activation(v[:, n, :, 0, :], g_bank[n % 2][:].rearrange("p (h d) -> p h d", d=HEAD),
                                       ACT.Copy).then_inc(vhi_made, 1)

                    def ot_halves(b, p):
                        act.wait_ge(pv_done, b * 8 + (2 * p + 1))
                        if not (isinstance(b, int) and b * PAIRS + p == 0):
                            act.wait_ge(otlo_made, b * 4 + p)
                        act.activation(ot[0:HEAD, :], o_bank[0][HEAD:P, :], ACT.Copy).then_inc(ot_half, 1)
                        act.wait_ge(pv_done, b * 8 + (2 * p + 2))
                        act.activation(ot[HEAD:P, :], o_bank[1][0:HEAD, :], ACT.Copy).then_inc(ot_half, 1)

                    def ot_hi_part(b, p):
                        act.wait_ge(ot_summed, b * 8 + (2 * p + 2))
                        if p == 0 and not (isinstance(b, int) and b == 0):
                            act.wait_ge(proj_done, b * 4)
                        act.activation(ot_hi[:, p, :], ot[:], ACT.Copy).then_inc(othi_made, 1)

                    def result(b, n):
                        act.wait_ge(shift_made, b * 4 + (n - 3))
                        act.activation(o[:, n, :], rows_of(b, n)[0], ACT.Identity, bias=shift[:, n:n + 1],
                                       scale=rstd[:, n, 1:2]).then_inc(y_made, 1)

                    def unit_hi(b, k, i, more):
                        if k // T == 0:
                            v_hi_part(b, i)
                        elif k // T >= 2 and more:
                            qk_hi_part(b + 1, (k // T - 2) * 4 + i)

                    def batch(b, last_part=True, more=True):
                        for k in range(STEPS):
                            if k == 3:
                                unit_hi(b, k, 3, more)
                            pt_hi_part(b, k)
                            if k % T == 3 and k > 3:
                                unit_hi(b, k, 3, more)
                            if last_part and row_at(k - 2, LN_STEP) is not None:
                                result(b, row_at(k - 2, LN_STEP))
                            for j, stage_of in ((0, ot_halves), (2, ot_hi_part)):
                                if output_at(b, k, j) and (last_part or k >= T):
                                    stage_of(*output_at(b, k, j))
                            if k + 2 < STEPS or more:
                                exponent(b, k + 2)
                            if k % T < 3:
                                unit_hi(b, k, k % T, more)

                    for i in range(2 * PAIRS):
                        qk_hi_part(0, i)
                    exponent(0, 0)
                    exponent(0, 1)
                    batch(0, last_part=False)
                    with act.Fori(1, B - 1, 1) as b:
                        batch(b)
                    batch(B - 1, more=False)
                    ot_halves(B - 1, PAIRS - 1)
                    ot_hi_part(B - 1, PAIRS - 1)
                    for n in range(T):
                        result(B, n)

                @block.vector
                def _(dve):
                    def masked_max(b, k, waited=False):
                        if not waited:
                            dve.wait_ge(scores_made, b * 32 + (2 * k + 2))
                        for a in range(2):
                            dve.tensor_tensor_reduce(probs[:, k % 2, a, :], s_bank[a][:], mask_bias[:, k % T, :],
                                                     -SCALE, 3.0e38, ALU.add, ALU.min,
                                                     bias_row[:, k % 4, a:a + 1]).then_inc(max_found, 1)

                    def inverse(b, k):
                        dve.wait_ge(exp_made, b * 32 + (2 * k + 2))
                        dve.reciprocal(inv_sums[:, k % 4, :], sums[:, k % 4, :]).then_inc(inv_made, 1)

                    def pt_lo_part(b, k, scores_too):
                        cols = slice(k % T * P, (k % T + 1) * P)
                        for a in range(2):
                            dve.wait_ge(pthi_made, b * 32 + (2 * k + a + 1))
                            if a == 1 and scores_too:
                                dve.wait_ge(scores_made, b * 32 + (2 * k + 6))
                            dve.tensor_tensor(pt_lo[:, a, :, cols], t_bank[a][:].rearrange("p (m n) -> p m n", m=T),
                                              f32(pt_hi[:, a, :, cols]), ALU.subtract).then_inc(ptlo_made, 1)

                    def qk_lo_part(b, i):
                        dve.wait_ge(qkhi_made, b * 8 + (i + 1))
                        hi, lo = ((q_hi, q_lo), (k_hi, k_lo))[i % 2]
                        dve.tensor_tensor(lo[:, i // 2, :], g_bank[i % 2][:], f32(hi[:, i // 2, :]), ALU.subtract)\
                            .then_inc(qklo_made, 1)

                    def v_lo_part(b, n):
                        dve.wait_ge(vhi_made, b * 4 + (n + 1))
                        dve.tensor_tensor(v[:, n, :, 1, :], g_bank[n % 2][:].rearrange("p (h d) -> p h d", d=HEAD),
                                          f32(v[:, n, :, 0, :]), ALU.subtract).then_inc(vlo_made, 1)

                    def ot_sum(b, p):
                        for a in range(2):
                            dve.wait_ge(ot_half, b * 8 + (2 * p + a + 1))
                            h = slice(a * HEAD, (a + 1) * HEAD)
                            dve.tensor_tensor(ot[h, :], o_bank[a][h, :], ot[h, :], ALU.add).then_inc(ot_summed, 1)

                    def ot_lo_part(b, p):
                        dve.wait_ge(othi_made, b * 4 + (p + 1))
                        dve.tensor_tensor(ot_lo[:, p, :], ot[:], f32(ot_hi[:, p, :]), ALU.subtract)\
                            .then_inc(otlo_made, 1)

                    def statistics(b, n, i, rows_of):
                        dve.bn_stats(stats[:, n, i, :], rows_of).then_inc(stats_made[i], 1)
                        dve.wait_ge(stats_made[i], 1)
                        dve.wait_ge(stats_made[i], b * 4 + (n - 3))
                        dve.bn_aggr(mean_var[:, n, i, :], stats[:, n, i, :]).then_inc(mean_made[i], 1)
                        dve.wait_ge(mean_made[i], b * 4 + (n - 3))
                        dve.tensor_scalar(var_eps[:, n, i:i + 1], mean_var[:, n, i, 1:2], EPS, None, ALU.add)\
                            .then_inc(eps_added[i], 1)

                    def row_shift(b, n):
                        dve.wait_ge(rstd_made[1], b * 4 + (n - 3))
                        dve.tensor_scalar(shift[:, n:n + 1], mean_var[:, n, 1, 0:1], rstd[:, n, 1:2], -1.0,
                                          ALU.mult, ALU.mult).then_inc(shift_made, 1)

                    def add_bproj(b, n):
                        dve.wait_ge(proj_done, b * 4 + (n - 3))
                        if n == 0 and not (isinstance(b, int) and b == 1):
                            dve.wait_ge(y_stored, b * 64 - 64)
                        dve.tensor_tensor(o[:, n, :], g_bank[n % 2][:], bproj_row[:], ALU.add).then_inc(o_made, 1)

                    def first_statistics(b, n):
                        dve.wait_ge(o_made, b * 4 + (n - 3))
                        statistics(b, n, 0, o[:, n, :])

                    def add_layernorm(b, n):
                        t_row = rows_of(b, n)[0]
                        if not (isinstance(b, int) and (b == B or (b == 1 and n == 0))):
                            dve.wait_ge(y_made, b * 4 + (n - 4))
                        dve.scalar_tensor_tensor(out=t_row, in0=o[:, n, :], scalar=mean_var[:, n, 0, 0:1],
                                                 in1=gamma_row[:], op0=ALU.subtract, op1=ALU.mult)\
                            .then_inc(gamma_done, 1)
                        dve.wait_ge(rstd_made[0], b * 4 + (n - 3))
                        dve.wait_ge(gamma_done, b * 4 + (n - 3))
                        dve.scalar_tensor_tensor(out=t_row, in0=t_row, scalar=rstd[:, n, 0:1], in1=o[:, n, :],
                                                 op0=ALU.mult, op1=ALU.add).then_inc(o_added, 1)

                    def last_statistics(b, n):
                        dve.wait_ge(u_added, b * 4 + (n - 3))
                        statistics(b, n, 1, rows_of(b, n)[0])

                    def unit_lo(b, k, i, more):
                        if k // T == 0:
                            v_lo_part(b, i)
                        elif k // T >= 2 and more:
                            qk_lo_part(b + 1, (k // T - 2) * 4 + i)

                    def batch(b, last_part=True, more=True):
                        for k in range(STEPS):
                            ahead = k + 2 < STEPS or more
                            if k + 1 < STEPS or more:
                                inverse(b, k + 1)
                            if k % T in (1, 2):
                                unit_lo(b, k, k % T - 1, more)
                            elif k == 3:
                                unit_lo(b, k, 3, more)
                            if last_part and k == O_STEP[3]:
                                add_bproj(b, 3)
                            pt_lo_part(b, k, ahead)
                            if last_part and row_at(k - 2, LN_STEP) is not None:
                                row_shift(b, row_at(k - 2, LN_STEP))
                            if ahead:
                                masked_max(b, k + 2, waited=True)
                            for j, stage_of in ((1, ot_sum), (2, ot_lo_part)):
                                if output_at(b, k, j) and (last_part or k >= T):
                                    stage_of(*output_at(b, k, j))
                            if last_part and row_at(k, O_STEP) is not None:
                                if k != O_STEP[3]:
                                    add_bproj(b, row_at(k, O_STEP))
                                first_statistics(b, row_at(k, O_STEP))
                            if last_part and row_at(k - 1, LN_STEP) is not None:
                                last_statistics(b, row_at(k - 1, LN_STEP))
                            if last_part and row_at(k, LN_STEP) is not None:
                                add_layernorm(b, row_at(k, LN_STEP))
                            if k % T == 2 or (k % T == 3 and k > 3):
                                unit_lo(b, k, k % T, more)

                    for i in range(2 * PAIRS):
                        qk_lo_part(0, i)
                    masked_max(0, 0)
                    masked_max(0, 1)
                    inverse(0, 0)
                    batch(0, last_part=False)
                    batch(1)
                    with dve.Fori(2, B - 1, 1) as b:
                        batch(b)
                    batch(B - 1, more=False)
                    ot_sum(B - 1, PAIRS - 1)
                    ot_lo_part(B - 1, PAIRS - 1)
                    for i in range(T + 3):
                        if i < T:
                            add_bproj(B, i)
                            first_statistics(B, i)
                        if 0 <= i - 1 < T:
                            add_layernorm(B, i - 1)
                        if 0 <= i - 2 < T:
                            last_statistics(B, i - 2)
                        if 0 <= i - 3 < T:
                            row_shift(B, i - 3)


_INS = ["x", "adj", "L0_gnn_weight", "L0_gnn_bias", "L1_gnn_w_qkv", "L1_gnn_w_proj", "L1_gnn_b_proj",
        "L1_gnn_ln_gamma", "L1_gnn_ln_beta"]


def kernel(**inputs):
    import numpy as _np
    import concourse.bacc as _bacc
    from concourse import mybir as _mybir
    from concourse.bass_utils import run_bass_kernel_spmd as _run

    nc = _bacc.Bacc("TRN2", target_bir_lowering=False, num_devices=1)
    arrays, args = {}, []
    for name in _INS:
        a = _np.ascontiguousarray(inputs[name])
        arrays[f"in_{name}_dram"] = a
        args.append(nc.dram_tensor(f"in_{name}_dram", a.shape, _mybir.dt.from_np(a.dtype), kind="ExternalInput").ap())
    shape = arrays["in_x_dram"].shape
    out = nc.dram_tensor("out_0_dram", shape, _mybir.dt.float32, kind="ExternalOutput").ap()
    graph_layers(nc, *args, out)
    r = _run(nc, [arrays], core_ids=[0])
    return r.results[0]["out_0_dram"]
```
